# Optimizing a Trainium2 kernel written in Bass

```python
import numpy as np
import jax
import jax.numpy as jnp

def _softmax(x, axis=-1):
    return jax.nn.softmax(x, axis=axis)

def _gelu(x):
    return jax.nn.gelu(x, approximate=True)

def _silu(x):
    return jax.nn.silu(x)

def _sigmoid(x):
    return jax.nn.sigmoid(x)

def _layernorm(x, axis=-1, eps=1e-05):
    m = jnp.mean(x, axis=axis, keepdims=True)
    v = jnp.var(x, axis=axis, keepdims=True)
    return (x - m) / jnp.sqrt(v + eps)

def _scatter_add(tgt, idx, src, axis=0):
    return tgt.at[idx].add(src)

def _segment_sum(src, seg, n):
    return jax.ops.segment_sum(src, seg, n)
kernel_name = 'mk_flamingo_gated_d1_seqx_r2_fcca64'

def setup_inputs(seed: int=0):
    np.random.seed(seed)
    _w = jnp.asarray

    def _rec_inputs():
        import jax
        import jax.numpy as jnp
        _rk = jax.random.key(seed)
        x = -0.0002928 + 1 * jax.random.normal(jax.random.fold_in(_rk, 1), (8, 512, 1024), jnp.float32)
        _lenS = 512 - jax.random.randint(jax.random.fold_in(_rk, 7), (8,), 0, max(1, 512 // 4) + 1, jnp.int32)
        _lenS2 = 512 - jax.random.randint(jax.random.fold_in(_rk, 8), (8,), 0, max(1, 512 // 4) + 1, jnp.int32)
        _ctx_2048P = jax.random.normal(jax.random.fold_in(_rk, 11), (8, 16, 1024), jnp.float32)
        _ctx_2048c = jax.random.dirichlet(jax.random.fold_in(_rk, 511), 0.3 * jnp.ones((16,), jnp.float32), (8, 512))
        _ctx_2048t = jnp.einsum('bsk,bkd->bsd', _ctx_2048c, _ctx_2048P)
        _ctx_2048t = _ctx_2048t * jax.lax.rsqrt(jnp.mean(jnp.square(_ctx_2048t)) + 1e-12) * 0.953939
        ctx_2048 = -1.39393e-06 + 0.999914 * (_ctx_2048t + 0.3 * jax.random.normal(jax.random.fold_in(_rk, 611), (8, 512, 1024), jnp.float32))
        _g = jax.random.normal(jax.random.fold_in(_rk, 9001), (2, 1), jnp.float32)
        _g = jnp.sign(_g) * jnp.maximum(jnp.abs(_g), 1.0) + (_g == 0) * 1.0
        g_xattn = _g[0]
        g_ffn = _g[1]
        return (x, ctx_2048, g_xattn, g_ffn)
    x, ctx_2048, g_xattn, g_ffn = _rec_inputs()

    def _L0_xattn_setup():
        import jax, jax.numpy as jnp
        import numpy as np
        B, S, E, NH = (2, 512, 1024, 16)
        DH = E // NH
        EPS = 1e-06

        def _mlstm_forward(q, k, v, Wi, bi, Wf, bf, ln_scale):
            b, s, e = q.shape
            nh = Wi.shape[1]
            dh = e // nh
            x = jnp.concatenate([q, k, v], axis=-1)
            ig = (x @ Wi + bi).transpose(0, 2, 1)[..., None]
            fg = (x @ Wf + bf).transpose(0, 2, 1)[..., None]
            split = lambda t: t.reshape(b, s, nh, dh).transpose(0, 2, 1, 3)
            qh, kh, vh = (split(q), split(k), split(v))
            log_f = jax.nn.log_sigmoid(fg)
            log_f_cum = jnp.concatenate([jnp.zeros((b, nh, 1, 1), q.dtype), jnp.cumsum(log_f, axis=2)], axis=2)
            fg_mat = log_f_cum - jnp.transpose(log_f_cum, (0, 1, 3, 2))
            ltr = jnp.tril(jnp.ones((s, s), dtype=bool))
            log_fg = jnp.where(ltr, fg_mat[:, :, 1:, 1:], -jnp.inf)
            log_D = log_fg + jnp.transpose(ig, (0, 1, 3, 2))
            max_log_D = jnp.max(log_D, axis=-1, keepdims=True)
            D = jnp.exp(log_D - max_log_D)
            qk = jnp.einsum('bhsd,bhtd->bhst', qh, kh) / jnp.sqrt(jnp.asarray(dh, q.dtype))
            C = qk * D
            normalizer = jnp.maximum(jnp.abs(C.sum(-1, keepdims=True)), jnp.exp(-max_log_D))
            Cn = C / (normalizer + EPS)
            h = jnp.einsum('bhst,bhtd->bhsd', Cn, vh)
            mu = h.mean(-1, keepdims=True)
            var = ((h - mu) ** 2).mean(-1, keepdims=True)
            hn = (h - mu) * jax.lax.rsqrt(var + EPS)
            hn = hn * ln_scale.reshape(1, nh, 1, dh)
            return hn.transpose(0, 2, 1, 3).reshape(b, s, e)
        key = jax.random.key(seed)
        ks = jax.random.split(key, 6)
        q = jax.random.normal(ks[0], (B, S, E), dtype=jnp.float32)
        k = jax.random.normal(ks[1], (B, S, E), dtype=jnp.float32)
        v = jax.random.normal(ks[2], (B, S, E), dtype=jnp.float32)
        Wi = jax.random.normal(ks[3], (3 * E, NH), dtype=jnp.float32) * 0.02
        bi = jax.random.normal(ks[4], (NH,), dtype=jnp.float32) * 0.1
        Wf = jax.random.normal(ks[5], (3 * E, NH), dtype=jnp.float32) * 0.02
        bf = jnp.linspace(3.0, 6.0, NH, dtype=jnp.float32)
        ln_scale = jnp.ones((E,), dtype=jnp.float32)
        return {'q': q, 'k': k, 'v': v, 'Wi': Wi, 'bi': bi, 'Wf': Wf, 'bf': bf, 'ln_scale': ln_scale}
    _L0_xattn_all = _L0_xattn_setup()
    _L0_xattn_in = {k: v for k, v in _L0_xattn_all.items() if k in ('Wi', 'bi', 'Wf', 'bf', 'ln_scale')}
    del _L0_xattn_all

    def _L0_ffn_setup():
        import jax, jax.numpy as jnp
        import numpy as np
        B, S, D = (2, 1024, 1024)
        E, TOP_K = (16, 2)
        F_EXP, F_SH = (512, 1024)

        def _reference_tuple_inner(hidden_states, router_w, gate_w, up_w, down_w, shared_gate_w, shared_up_w, shared_down_w):
            b, s, d = hidden_states.shape
            flat = hidden_states.reshape(-1, d)
            T = flat.shape[0]
            router_logits = flat @ router_w.T
            probs = jax.nn.softmax(router_logits, axis=-1)
            topk_w, topk_idx = jax.lax.top_k(probs, TOP_K)
            topk_w = topk_w / jnp.sum(topk_w, axis=-1, keepdims=True)
            shared = jax.nn.silu(flat @ shared_gate_w) * (flat @ shared_up_w) @ shared_down_w
            flat_idx = topk_idx.reshape(-1)
            flat_w = topk_w.reshape(-1)
            token_ids = jnp.repeat(jnp.arange(T), TOP_K)
            order = jnp.argsort(flat_idx)
            sorted_tok = token_ids[order]
            sorted_w = flat_w[order]
            group_sizes = jnp.bincount(flat_idx, length=E).astype(jnp.int32)
            xs = flat[sorted_tok]
            g = jax.lax.ragged_dot(xs, gate_w, group_sizes)
            u = jax.lax.ragged_dot(xs, up_w, group_sizes)
            h = jax.nn.silu(g) * u
            dn = jax.lax.ragged_dot(h, down_w, group_sizes)
            routed = jnp.zeros_like(flat).at[sorted_tok].add(sorted_w[:, None] * dn)
            output = (shared + routed).reshape(b, s, d)
            return (output, router_logits)
        key = jax.random.key(seed)
        ks = jax.random.split(key, 8)
        scale = 0.02
        return {'hidden_states': jax.random.normal(ks[0], (B, S, D), jnp.float32), 'router_w': jax.random.normal(ks[1], (E, D), jnp.float32) * scale, 'gate_w': jax.random.normal(ks[2], (E, D, F_EXP), jnp.float32) * scale, 'up_w': jax.random.normal(ks[3], (E, D, F_EXP), jnp.float32) * scale, 'down_w': jax.random.normal(ks[4], (E, F_EXP, D), jnp.float32) * scale, 'shared_gate_w': jax.random.normal(ks[5], (D, F_SH), jnp.float32) * scale, 'shared_up_w': jax.random.normal(ks[6], (D, F_SH), jnp.float32) * scale, 'shared_down_w': jax.random.normal(ks[7], (F_SH, D), jnp.float32) * scale}
    _L0_ffn_all = _L0_ffn_setup()
    _L0_ffn_in = {k: v for k, v in _L0_ffn_all.items() if k in ('router_w', 'gate_w', 'up_w', 'down_w', 'shared_gate_w', 'shared_up_w', 'shared_down_w')}
    del _L0_ffn_all
    return {'x': x, 'ctx_2048': ctx_2048, 'g_xattn': g_xattn, 'g_ffn': g_ffn, 'L0_xattn_Wi': _L0_xattn_in['Wi'], 'L0_xattn_bi': _L0_xattn_in['bi'], 'L0_xattn_Wf': _L0_xattn_in['Wf'], 'L0_xattn_bf': _L0_xattn_in['bf'], 'L0_xattn_ln_scale': _L0_xattn_in['ln_scale'], 'L0_ffn_router_w': _L0_ffn_in['router_w'], 'L0_ffn_gate_w': _L0_ffn_in['gate_w'], 'L0_ffn_up_w': _L0_ffn_in['up_w'], 'L0_ffn_down_w': _L0_ffn_in['down_w'], 'L0_ffn_shared_gate_w': _L0_ffn_in['shared_gate_w'], 'L0_ffn_shared_up_w': _L0_ffn_in['shared_up_w'], 'L0_ffn_shared_down_w': _L0_ffn_in['shared_down_w']}

def reference(x, ctx_2048, g_xattn, g_ffn, L0_xattn_Wi, L0_xattn_bi, L0_xattn_Wf, L0_xattn_bf, L0_xattn_ln_scale, L0_ffn_router_w, L0_ffn_gate_w, L0_ffn_up_w, L0_ffn_down_w, L0_ffn_shared_gate_w, L0_ffn_shared_up_w, L0_ffn_shared_down_w):
    import jax
    import jax.numpy as jnp

    def _L0_xattn_ref(q, k, v, Wi, bi, Wf, bf, ln_scale):
        import jax, jax.numpy as jnp
        import numpy as np
        B, S, E, NH = (2, 512, 1024, 16)
        DH = E // NH
        EPS = 1e-06

        def _mlstm_forward(q, k, v, Wi, bi, Wf, bf, ln_scale):
            b, s, e = q.shape
            nh = Wi.shape[1]
            dh = e // nh
            x = jnp.concatenate([q, k, v], axis=-1)
            ig = (x @ Wi + bi).transpose(0, 2, 1)[..., None]
            fg = (x @ Wf + bf).transpose(0, 2, 1)[..., None]
            split = lambda t: t.reshape(b, s, nh, dh).transpose(0, 2, 1, 3)
            qh, kh, vh = (split(q), split(k), split(v))
            log_f = jax.nn.log_sigmoid(fg)
            log_f_cum = jnp.concatenate([jnp.zeros((b, nh, 1, 1), q.dtype), jnp.cumsum(log_f, axis=2)], axis=2)
            fg_mat = log_f_cum - jnp.transpose(log_f_cum, (0, 1, 3, 2))
            ltr = jnp.tril(jnp.ones((s, s), dtype=bool))
            log_fg = jnp.where(ltr, fg_mat[:, :, 1:, 1:], -jnp.inf)
            log_D = log_fg + jnp.transpose(ig, (0, 1, 3, 2))
            max_log_D = jnp.max(log_D, axis=-1, keepdims=True)
            D = jnp.exp(log_D - max_log_D)
            qk = jnp.einsum('bhsd,bhtd->bhst', qh, kh) / jnp.sqrt(jnp.asarray(dh, q.dtype))
            C = qk * D
            normalizer = jnp.maximum(jnp.abs(C.sum(-1, keepdims=True)), jnp.exp(-max_log_D))
            Cn = C / (normalizer + EPS)
            h = jnp.einsum('bhst,bhtd->bhsd', Cn, vh)
            mu = h.mean(-1, keepdims=True)
            var = ((h - mu) ** 2).mean(-1, keepdims=True)
            hn = (h - mu) * jax.lax.rsqrt(var + EPS)
            hn = hn * ln_scale.reshape(1, nh, 1, dh)
            return hn.transpose(0, 2, 1, 3).reshape(b, s, e)
        return _mlstm_forward(q, k, v, Wi, bi, Wf, bf, ln_scale)

    def _L0_ffn_ref(hidden_states, router_w, gate_w, up_w, down_w, shared_gate_w, shared_up_w, shared_down_w):
        import jax, jax.numpy as jnp
        import numpy as np
        B, S, D = (2, 1024, 1024)
        E, TOP_K = (16, 2)
        F_EXP, F_SH = (512, 1024)

        def _reference_tuple_inner(hidden_states, router_w, gate_w, up_w, down_w, shared_gate_w, shared_up_w, shared_down_w):
            b, s, d = hidden_states.shape
            flat = hidden_states.reshape(-1, d)
            T = flat.shape[0]
            router_logits = flat @ router_w.T
            probs = jax.nn.softmax(router_logits, axis=-1)
            topk_w, topk_idx = jax.lax.top_k(probs, TOP_K)
            topk_w = topk_w / jnp.sum(topk_w, axis=-1, keepdims=True)
            shared = jax.nn.silu(flat @ shared_gate_w) * (flat @ shared_up_w) @ shared_down_w
            flat_idx = topk_idx.reshape(-1)
            flat_w = topk_w.reshape(-1)
            token_ids = jnp.repeat(jnp.arange(T), TOP_K)
            order = jnp.argsort(flat_idx)
            sorted_tok = token_ids[order]
            sorted_w = flat_w[order]
            group_sizes = jnp.bincount(flat_idx, length=E).astype(jnp.int32)
            xs = flat[sorted_tok]
            g = jax.lax.ragged_dot(xs, gate_w, group_sizes)
            u = jax.lax.ragged_dot(xs, up_w, group_sizes)
            h = jax.nn.silu(g) * u
            dn = jax.lax.ragged_dot(h, down_w, group_sizes)
            routed = jnp.zeros_like(flat).at[sorted_tok].add(sorted_w[:, None] * dn)
            output = (shared + routed).reshape(b, s, d)
            return (output, router_logits)
        return _reference_tuple_inner(hidden_states, router_w, gate_w, up_w, down_w, shared_gate_w, shared_up_w, shared_down_w)[0]
    x = x + jnp.tanh(g_xattn[0]) * _L0_xattn_ref(_layernorm(x, axis=-1), ctx_2048, ctx_2048, L0_xattn_Wi, L0_xattn_bi, L0_xattn_Wf, L0_xattn_bf, L0_xattn_ln_scale)
    x = x + jnp.tanh(g_ffn[0]) * _L0_ffn_ref(_layernorm(x, axis=-1), L0_ffn_router_w, L0_ffn_gate_w, L0_ffn_up_w, L0_ffn_down_w, L0_ffn_shared_gate_w, L0_ffn_shared_up_w, L0_ffn_shared_down_w)
    return x

_drawn_inputs = setup_inputs


def setup_inputs(seed=0):
    import zlib

    import numpy as np

    out = dict(_drawn_inputs(seed))
    spreads = {'L0_xattn_ln_scale': (1.0, 0.2)}
    factors = {'L0_xattn_bi': 64.0}
    for name, (base, spread) in spreads.items():
        noise = np.random.default_rng([zlib.crc32(name.encode()), seed]).standard_normal(out[name].shape)
        drawn = base * np.exp(spread * noise) if base else spread * noise
        out[name] = jnp.asarray(drawn.astype(out[name].dtype))
    for name, factor in factors.items():
        out[name] = (out[name] * factor).astype(out[name].dtype)
    return out
```

```python
from contextlib import ExitStack

import numpy as np

import concourse.bass as bass
from concourse import mybir
from concourse.alu_op_type import AluOpType as ALU

P = 128
B, S, D = 8, 512, 1024
T = B * S
NH, DH = 16, 64
NE, FE, FS = 16, 512, 1024
KD = D // P
NCH = T // P
CPB = S // P
HV = DH + 1
HG = 4
NG = NH // HG
LN_EPS, H_EPS = 1e-5, 1e-6
MIN_TILES = 2
MAX_TILES = 2 * T // P + MIN_TILES * NE + 2
CAP = T
PIECES = 12
GUP = 8
DVE_HI = 2
NEG = -3.0e38
DVE_PER_BATCH = 146


def ge(eng, sem, n):
    if isinstance(n, int) and n <= 0:
        return
    eng.wait_ge(sem, n)


def ge_apart(eng, past, *waits):
    for sem, n in waits:
        ge(eng, sem, n)
    eng.sem_inc(past, 1)


class Chain:

    def __init__(self, eng, sem):
        self.eng, self.sem, self.base, self.n = eng, sem, 0, 0

    def step(self, ins):
        ins.then_inc(self.sem, 1)
        self.n += 1

    def settle(self):
        self.eng.wait_ge(self.sem, self.base + self.n)

    def settle_apart(self, past):
        ge_apart(self.eng, past, (self.sem, self.base + self.n))

    def link(self, ins):
        self.step(ins)
        self.settle()


def mix_block(nc, t, keep):
    f32, f32r, i32, u32 = mybir.dt.float32, mybir.dt.float32r, mybir.dt.int32, mybir.dt.uint32
    ACT, AX = mybir.ActivationFunctionType, mybir.AxisListType
    with ExitStack() as ctx:
        def sb(name, shape, dt=f32):
            return ctx.enter_context(nc.sbuf_tensor(name, shape, dt))

        def pb(name, shape, dt=f32):
            return ctx.enter_context(nc.psum_tensor(name, shape, dt))

        def sem(name):
            return ctx.enter_context(nc.semaphore(name))

        ident = keep["ident"]
        upper = sb("upper", [P, P])
        ones = sb("ones", [P, P])
        headsel = sb("headsel", [NH, P])
        headmask = sb("headmask", [NH, KD])
        one_row = sb("one_row", [NH, P])
        zero_row = sb("zero_row", [NH, P])
        w_gate = sb("w_gate", [P, 3 * KD, 2 * NH])
        gate_bias = sb("gate_bias", [P, 2 * NH])
        rw = sb("rw", [P, KD, NE])
        rw_hi, rw_lo = sb("rw_hi", [P, KD, NE], f32r), sb("rw_lo", [P, KD, NE], f32r)
        lns = sb("lns", [P, D])
        gx = sb("gx", [P, 2])
        iota_e = keep["iota_e"]
        tok_all = sb("tok_all", [P, NCH], i32)
        zero_i = sb("zero_i", [P, (NE * CAP + P) // P], i32)
        mhalf = sb("mhalf", [P, NH])
        x = sb("x", [P, 4, D])
        ctx_t = sb("ctx_t", [P, 4, KD, P])
        ctx_v = sb("ctx_v", [P, 2, NH, HV])
        q = sb("q", [P, NH, DH])
        q_t = sb("q_t", [P, 2, KD, P])
        qs = sb("qs", [P, NH, DH])
        qs_t = sb("qs_t", [P, KD, P])
        gb = sb("gb", [P, NH, P])
        dmat = sb("dmat", [P, NH, P])
        ks = sb("ks", [P, NH, DH])
        cmat = sb("cmat", [P, 2, HG, P])
        uc = sb("uc", [P, 2, NH, HV])
        state = sb("state", [P, KD, HV])
        sq = sb("sq", [P, NH, DH])
        x1 = sb("x1", [P, 2, D])
        xn = sb("xn", [P, 2, D])
        xn_hi, xn_lo = sb("xn_hi", [P, KD, P], f32r), sb("xn_lo", [P, KD, P], f32r)
        st1, mv1, rs1 = sb("st1", [P, 2, 6]), sb("mv1", [P, 2]), sb("rs1", [P, 2])
        st2, mv2, rs2 = sb("st2", [P, 2, 6]), sb("mv2", [P, 2]), sb("rs2", [P, 2])
        gates = sb("gates", [P, 2 * NH])
        absf, lnf = sb("absf", [P, NH]), sb("lnf", [P, 2, NH])
        fcum = sb("fcum", [NH, 2, P])
        gmax = sb("gmax", [NH, 2, P])
        rows = sb("rows", [NH, 4, P])
        neg_g = sb("neg_g", [NH, P])
        dec = sb("dec", [NH, 2])
        decm = sb("decm", [NH, KD])
        cols = sb("cols", [P, 4, 4, NH])
        qfac = sb("qfac", [P, NH])
        nrm, mu, var = sb("nrm", [P, 2, NH]), sb("mu", [P, 2, NH]), sb("var", [P, 3, NH])
        lg, mx, ix = sb("lg", [P, NE]), sb("mx", [P, 8]), sb("ix", [P, 8], u32)
        hot = sb("hot", [P, 3, NE])
        hot_acc = keep["hot_acc"]
        scr = sb("scr", [P, 2, NE])
        posf, posi = sb("posf", [P, 2]), sb("posi", [P, 2, 2], i32)
        tok = sb("tok", [P, 2], i32)
        ew = sb("ew", [P, 3])
        eidx, rank, wts = keep["eidx"], keep["rank"], keep["wts"]
        p_tr = [pb(f"p_tr{n}", [P, 4, P]) for n in range(2)]
        p_sc = pb("p_sc", [P, HG, P])
        p_u = [pb(f"p_u{n}", [P, 512]) for n in range(2)]
        p_gate = pb("p_gate", [P, 512])
        p_row = pb("p_row", [P, 512])
        p_rt = pb("p_rt", [P, 512])

        past = sem("past")
        const_in, table_in, scat0, scat1 = sem("const_in"), sem("table_in"), sem("scat0"), sem("scat1")
        x_in = [sem(f"x_in{n}") for n in range(4)]
        ct_in = [sem(f"ct_in{n}") for n in range(4)]
        cv_in = [sem(f"cv_in{n}") for n in range(2)]
        g_out, gb_in = sem("g_out"), sem("gb_in")
        x1_out = [sem(f"x1_out{n}") for n in range(2)]
        xn_out = [sem(f"xn_out{n}") for n in range(2)]
        pool_set, dve_set, act_set = sem("pool_set"), sem("dve_set"), sem("act_set")
        dve_steps, pool_steps = sem("dve_steps"), sem("pool_steps")
        var1, rs1_rdy, q_rdy = sem("var1"), sem("rs1_rdy"), sem("q_rdy")
        tr_ps, tr_sb = sem("tr_ps"), sem("tr_sb")
        gates_ps, absf_rdy, lnf_rdy, lf_rdy = sem("gates_ps"), sem("absf_rdy"), sem("lnf_rdy"), sem("lf_rdy")
        gt_ps, neg_g_rdy, rows_rdy, cols_ps, cols_rdy = (sem("gt_ps"), sem("neg_g_rdy"), sem("rows_rdy"),
                                                         sem("cols_ps"), sem("cols_rdy"))
        dec_rdy, decm_rdy, dec_ps = sem("dec_rdy"), sem("decm_rdy"), sem("dec_ps")
        qs_rdy, gb_rdy, d_rdy, ks_rdy = sem("qs_rdy"), sem("gb_rdy"), sem("d_rdy"), sem("ks_rdy")
        sc_ps, c_rdy, u_ps, u_rdy, ds_ps, state_rdy = (
            sem("sc_ps"), sem("c_rdy"), sem("u_ps"), sem("u_rdy"), sem("ds_ps"), sem("state_rdy"))
        cen_rdy, sq_rdy, var_rdy, hrs_rdy, o_rdy, x1_rdy = (
            sem("cen_rdy"), sem("sq_rdy"), sem("var_rdy"), sem("hrs_rdy"), sem("o_rdy"), sem("x1_rdy"))
        var2, rs2_rdy, xn_rdy, hi_rdy, lo_rdy = sem("var2"), sem("rs2_rdy"), sem("xn_rdy"), sem("hi_rdy"), sem("lo_rdy")
        lg_ps, hot_rdy, rank_ps, pos_rdy = sem("lg_ps"), sem("hot_rdy"), sem("rank_ps"), sem("pos_rdy")
        top_rdy, ew_rdy = sem("top_rdy"), sem("ew_rdy")

        x_rows = t["x"].rearrange("(c p) d -> c p d", p=P)
        ctx_rows = t["ctx"].rearrange("(c p) (h d) -> c p h d", p=P, h=NH)
        x1_rows = t["x1"].rearrange("(c p) d -> c p d", p=P)
        xn_rows = t["xn"].rearrange("(c p) d -> c p d", p=P)

        def schedule(eng, chain, ahead, mid, behind, fori):
            def turn(b, j):
                nxt = (b, j + 1) if j + 1 < CPB else (b + 1, 0)
                prv = (b, j - 1) if j else (b - 1, CPB - 1)
                if isinstance(nxt[0], int) and nxt[0] >= B:
                    nxt = None
                if isinstance(prv[0], int) and prv[0] < 0:
                    prv = None
                for kind, part in (("A", 1), ("B", 1), ("A", 2), ("B", 2), ("C", 1), ("A", 3), ("C", 2)):
                    at = {"A": nxt, "B": (b, j), "C": prv}[kind]
                    fn = {"A": ahead, "B": mid, "C": behind}[kind]
                    if at is not None:
                        fn(part, *at)

            for part in (1, 2, 3):
                ahead(part, 0, 0)
            for j in range(CPB):
                turn(0, j)
            before = chain.n if chain else 0
            with fori(1, B - 1) as b:
                if chain:
                    chain.base = (b - 1) * chain.per
                for j in range(CPB):
                    turn(b, j)
                if chain:
                    assert chain.n - before == chain.per, (chain.n - before, chain.per)
            if chain:
                chain.base = (B - 3) * chain.per
            for j in range(CPB):
                turn(B - 1, j)
            for part in (1, 2):
                behind(part, B - 1, CPB - 1)

        def nothing(*_):
            pass

        def heads(g):
            return [8 * (g // 2) + g % 2 + 2 * n for n in range(HG)]

        def states_through(b, j, back):
            return (CPB - 1) * b + max(j + 1 - back, 0)

        order = [("q", 0)]
        for cc in range(NCH):
            if cc + 1 < NCH:
                order.append(("q", cc + 1))
                if (cc + 1) % CPB:
                    order.append(("qs", cc + 1))
            if cc:
                order.append(("xn", cc - 1))
        order.append(("xn", NCH - 1))
        place = {what: 2 * n for n, what in enumerate(order)}
        turned_per_batch = 2 * (3 * CPB - 1)
        for kind in ("q", "qs", "xn"):
            for cc in range(2 * CPB, NCH - CPB - 1):
                if (kind, cc) in place:
                    assert place[kind, cc] - place[kind, cc - CPB] == turned_per_batch

        def turn_count(kind, b, j):
            if isinstance(b, int):
                return place[kind, b * CPB + j]
            return (b - 1) * turned_per_batch + place[kind, CPB + j]

        def parted(m):
            copied = sum(2 for kind, _ in order[:m] if kind != "xn")
            return copied, 2 * m - copied

        def parted_by(kind, b, j, own):
            if isinstance(b, int):
                return parted(place[kind, b * CPB + j] // 2 + own)
            copied, split = parted(place[kind, CPB + j] // 2 + own)
            return (b - 1) * 2 * (2 * CPB - 1) + copied, (b - 1) * 2 * CPB + split


        block = ctx.enter_context(nc.Block())

        @block.sync
        def _(sp):
            def load_x(b, j):
                c = b * CPB + j
                ge(sp, x1_rdy, c - 3)
                sp.dma_start(x[:, j, :], x_rows[c]).then_inc(x_in[j], 16)
                ge(sp, u_ps, NG * (c - 3))
                sp.dma_start(ctx_t[:, j], t["ctx_t"][c]).then_inc(ct_in[j], 16)

            def load_v(b, j):
                c = b * CPB + j
                ge(sp, u_ps, NG * (c - 1))
                ge(sp, ds_ps, 2 * states_through(b, j, 2))
                sp.dma_start(ctx_v[:, j % 2, :, 0:DH], ctx_rows[c]).then_inc(cv_in[j % 2], 16)

            def ahead(part, b, j):
                c = b * CPB + j
                if part == 1:
                    if isinstance(c, int) and c == 0:
                        load_x(0, 0)
                        load_x(0, 1)
                    nb, nj = (b, j + 1) if j + 1 < CPB else (b + 1, 0)
                    if not (isinstance(nb, int) and nb >= B) and not (isinstance(c, int) and c == 0):
                        load_x(nb, nj)
                    load_v(b, j)
                if part == 2:
                    ge(sp, neg_g_rdy, c + 1)
                    sp.dma_start(t["g_row"], neg_g[:, :]).then_inc(g_out, 16)
                    sp.wait_ge(g_out, 16 * c + 16)
                    ge(sp, d_rdy, NH * c)
                    sp.dma_start(gb[:, :, :], t["g_row"].rearrange("h s -> (h s)").partition_broadcast(P)
                                 ).then_inc(gb_in, 16)

            def behind(part, b, j):
                c = b * CPB + j
                if part == 1:
                    ge(sp, x1_rdy, c + 1)
                    sp.dma_start(x1_rows[c], x1[:, j % 2, :]).then_inc(x1_out[j % 2], 16)
                if part == 2:
                    ge(sp, xn_rdy, c + 1)
                    sp.dma_start(xn_rows[c], xn[:, j % 2, :]).then_inc(xn_out[j % 2], 16)

            sp.dma_start(w_gate[:, :, :], t["w_gate"].rearrange("(k p) n -> p k n", p=P)).then_inc(const_in, 16)
            sp.dma_start(gate_bias[:, :], t["gate_bias"].partition_broadcast(P)).then_inc(const_in, 16)
            sp.dma_start(rw[:, :, :], t["rw"].rearrange("(k p) n -> p k n", p=P)).then_inc(const_in, 16)
            sp.dma_start(lns[:, :], t["ln_scale"].partition_broadcast(P)).then_inc(const_in, 16)
            sp.dma_start(gx[:, 0:1], t["g_xattn"].partition_broadcast(P)).then_inc(const_in, 16)
            sp.dma_start(gx[:, 1:2], t["g_ffn"].partition_broadcast(P)).then_inc(const_in, 16)
            sp.wait_ge(pool_set, 1)
            sp.dma_start(t["lists"].rearrange("(p n) o -> p (n o)", p=P), zero_i[:, :]).then_inc(table_in, 16)
            schedule(sp, None, ahead, nothing, behind, sp.Fori)
            for n in range(2):
                sp.wait_ge(x1_out[n], 16 * NCH // 2)
                sp.wait_ge(xn_out[n], 16 * NCH // 2)

        @block.gpsimd
        def _(pool):
            nc.gpsimd.memset(zero_i[:, :], 0).then_inc(pool_set, 1)
            nc.gpsimd.memset(ident[:, :], 0.0).then_inc(pool_set, 1)
            nc.gpsimd.memset(upper[:, :], 1.0).then_inc(pool_set, 1)
            nc.gpsimd.memset(headmask[:, :], 1.0).then_inc(pool_set, 1)
            nc.gpsimd.memset(mhalf[:, :], -0.5).then_inc(pool_set, 1)
            pool.wait_ge(pool_set, 5)
            nc.gpsimd.affine_select(out=ident[:, :], in_=ident[:, :], compare_op=ALU.not_equal, fill=1.0,
                                    base=0, pattern=[[-1, P]], channel_multiplier=1).then_inc(pool_set, 1)
            nc.gpsimd.affine_select(out=upper[:, :], in_=upper[:, :], compare_op=ALU.is_gt, fill=0.0,
                                    base=0, pattern=[[1, P]], channel_multiplier=-1).then_inc(pool_set, 1)
            nc.gpsimd.affine_select(out=headmask[:, :], in_=headmask[:, :], compare_op=ALU.is_ge, fill=0.0,
                                    base=0, pattern=[[-2, KD]], channel_multiplier=1).then_inc(pool_set, 1)
            pool.wait_ge(pool_set, 8)
            nc.gpsimd.affine_select(out=headmask[:, :], in_=headmask[:, :], compare_op=ALU.is_ge, fill=0.0,
                                    base=1, pattern=[[2, KD]], channel_multiplier=-1).then_inc(pool_set, 1)
            nc.gpsimd.iota(tok_all[:, :], pattern=[[P, NCH]], base=0, channel_multiplier=1).then_inc(pool_set, 1)
            nc.gpsimd.iota(iota_e[:, :], pattern=[[1, NE]], base=0, channel_multiplier=0,
                           allow_small_or_imprecise_dtypes=True).then_inc(pool_set, 1)
            pool.wait_ge(table_in, 16)

            def ahead(part, b, j):
                c = b * CPB + j
                if part == 1:
                    ge(pool, var1, c + 1)
                    nc.gpsimd.tensor_tensor(rs1[:, 1:2], rs1[:, 0:1], mhalf[:, 0:1], ALU.pow).then_inc(rs1_rdy, 1)
                if part == 3:
                    ge_apart(pool, past, (gb_in, 16 * c + 16))
                    nc.gpsimd.affine_select(out=gb[:, :, :], in_=gb[:, :, :], compare_op=ALU.is_ge, fill=-1.0e30,
                                            base=0, pattern=[[0, NH], [1, P]], channel_multiplier=-1
                                            ).then_inc(gb_rdy, 1)
                    if j < CPB - 1:
                        ge(pool, cols_rdy, 2 * c + 2)
                        pool.wait_ge(cv_in[j % 2], 16 * (2 * b + j // 2) + 16)
                        ge(pool, ds_ps, 2 * ((CPB - 1) * b + j))
                        nc.gpsimd.tensor_tensor(ks[:, :, :], ctx_v[:, j % 2, :, 0:DH],
                                                cols[:, j, 1, :, None].to_broadcast([P, NH, DH]),
                                                ALU.mult).then_inc(ks_rdy, 1)

            def behind(part, b, j):
                c = b * CPB + j
                if part == 1:
                    ge(pool, var_rdy, c + 1)
                    nc.gpsimd.tensor_tensor(var[:, 2, :], var[:, 1, :], mhalf[:, :], ALU.pow).then_inc(hrs_rdy, 1)
                    ge(pool, o_rdy, c + 1)
                    o = sq[:, :, :].rearrange("p h d -> p (h d)")
                    nc.gpsimd.tensor_tensor(o, o, lns[:, :], ALU.mult).then_inc(pool_steps, 1)
                    ge(pool, pool_steps, c + 1)
                    ge(pool, x1_out[j % 2], 16 * (2 * b + j // 2))
                    nc.gpsimd.tensor_tensor(x1[:, j % 2, :], x[:, j, :], o, ALU.add).then_inc(x1_rdy, 1)
                if part == 2:
                    ge(pool, var2, c + 1)
                    nc.gpsimd.tensor_tensor(rs2[:, 1:2], rs2[:, 0:1], mhalf[:, 0:1], ALU.pow).then_inc(rs2_rdy, 1)
                    ge(pool, pos_rdy, c + 1)
                    for k, done in ((0, scat0), (1, scat1)):
                        ge_apart(pool, past, (done, 16 * c))
                        nc.gpsimd.indirect_dma_start(
                            out=t["lists"], out_offset=bass.IndirectOffsetOnAxis(ap=posi[:, j % 2, k:k + 1], axis=0),
                            in_=tok[:, j % 2:j % 2 + 1], in_offset=None).then_inc(done, 16)

            schedule(pool, None, ahead, nothing, behind, pool.Fori)
            pool.wait_ge(scat0, 16 * NCH)
            pool.wait_ge(scat1, 16 * NCH)

        @block.scalar
        def _(act):
            act.wait_ge(const_in, 96)
            nc.scalar.activation(gx[:, :], gx[:, :], ACT.Tanh).then_inc(act_set, 1)
            act.wait_ge(act_set, 1)
            nc.scalar.activation(lns[:, :], lns[:, :], ACT.Copy, scale=gx[:, 0:1]).then_inc(act_set, 1)
            nc.scalar.activation(keep["tgf"][:, :], gx[:, 1:2], ACT.Copy).then_inc(act_set, 1)
            nc.scalar.activation(rw_hi[:, :, :], rw[:, :, :], ACT.Copy).then_inc(act_set, 1)

            def turned(before, n, dst):
                act.wait_ge(tr_ps, before + n + 1)
                nc.scalar.activation(dst, p_tr[n][:, :, :], ACT.Copy).then_inc(tr_sb, 1)

            def ahead(part, b, j):
                c = b * CPB + j
                if part == 1:
                    for n in range(2):
                        if n == 0:
                            ge(act, u_ps, NG * (c - 1))
                        turned(turn_count("q", b, j), n, q_t[:, j % 2, 4 * n:4 * n + 4, :])
                if part == 2:
                    ge(act, absf_rdy, c + 1)
                    nc.scalar.activation(lnf[:, 0, :], absf[:, :], ACT.Exp, scale=-1.0).then_inc(lnf_rdy, 1)
                    act.wait_ge(lnf_rdy, 2 * c + 1)
                    nc.scalar.activation(lnf[:, 1, :], lnf[:, 0, :], ACT.Ln, bias=1.0).then_inc(lnf_rdy, 1)
                    ge(act, cols_ps, c + 1)
                    nc.scalar.activation(cols[:, j, 0, :], p_row[:, 256:256 + NH], ACT.Copy).then_inc(cols_rdy, 1)
                    lo, hi = (1, 3) if j == 0 else (2, 4) if j == CPB - 1 else (1, 4)
                    nc.scalar.activation(cols[:, j, lo:hi, :].rearrange("p a h -> p (a h)"),
                                         p_row[:, 256 + lo * NH:256 + hi * NH], ACT.Exp).then_inc(cols_rdy, 1)
                    if 0 < j < CPB - 1:
                        act.wait_ge(rows_rdy, c + 1)
                        nc.scalar.activation(dec[:, 1:2], dec[:, 0:1], ACT.Exp).then_inc(dec_rdy, 1)
                if part == 3:
                    if j > 0:
                        for n in range(2):
                            if n == 0:
                                ge(act, u_ps, NG * c)
                            turned(turn_count("qs", b, j), n, qs_t[:, 4 * n:4 * n + 4, :])
                    ge(act, gb_rdy, c + 1)
                    act.wait_ge(cols_rdy, 2 * c + 2)
                    ge(act, c_rdy, NG * c)
                    for h in range(NH):
                        nc.scalar.activation(dmat[:, h, :], gb[:, h, :], ACT.Exp,
                                             bias=cols[:, j, 0, h:h + 1]).then_inc(d_rdy, 1)

            def mid(part, b, j):
                c = b * CPB + j
                for g in ((0,) if part == 1 else (1, 2, 3)):
                    act.wait_ge(u_ps, NG * c + g + 1)
                    ge(act, o_rdy, c - 1)
                    nc.scalar.activation(uc[:, j % 2, heads(g)[0]:heads(g)[-1] + 1:2, :],
                                         p_u[g % 2][:, 0:HG * HV].rearrange("p (h d) -> p h d", d=HV),
                                         ACT.Copy).then_inc(u_rdy, 1)

            def behind(part, b, j):
                c = b * CPB + j
                if part == 1:
                    act.wait_ge(cen_rdy, c + 1)
                    nc.scalar.activation(sq[:, :, :], uc[:, j % 2, :, 0:DH], ACT.Square).then_inc(sq_rdy, 1)
                if part == 2:
                    for n in range(2):
                        act.wait_ge(tr_ps, turn_count("xn", b, j) + n + 1)
                        ge(act, lg_ps, c)
                        nc.scalar.activation(xn_hi[:, 4 * n:4 * n + 4, :], p_tr[n][:, :, :], ACT.Copy).then_inc(hi_rdy, 1)
                    ge(act, top_rdy, c + 1)
                    nc.scalar.activation(ew[:, 1:2], ew[:, 0:1], ACT.Exp).then_inc(ew_rdy, 1)

            schedule(act, None, ahead, mid, behind, act.Fori)

        @block.vector
        def _(dve):
            chain = Chain(dve, dve_steps)
            chain.per = DVE_PER_BATCH
            step, settle, link = chain.step, chain.settle, chain.link

            nc.vector.memset(ones[:, :], 1.0).then_inc(dve_set, 1)
            nc.vector.memset(one_row[:, :], 1.0).then_inc(dve_set, 1)
            nc.vector.memset(zero_row[:, :], 0.0).then_inc(dve_set, 1)
            nc.vector.memset(hot_acc[:, :], 0.0).then_inc(dve_set, 1)
            for n in range(2):
                nc.vector.memset(ctx_v[:, n, :, DH:HV], 1.0).then_inc(dve_set, 1)
            dve.wait_ge(pool_set, 11)
            idv = ident[0:NH, 0:NH].rearrange("p (j o) -> p o j", o=2)
            nc.vector.tensor_reduce(out=headsel[:, 0:1], in_=idv[:, 0, :], axis=AX.X, op=ALU.add).then_inc(dve_set, 1)
            nc.vector.tensor_reduce(out=headsel[:, DH:DH + 1], in_=idv[:, 1, :], axis=AX.X, op=ALU.add).then_inc(dve_set, 1)
            dve.wait_ge(dve_set, 8)
            for o in (0, DH):
                nc.vector.tensor_copy(headsel[:, o + 1:o + DH], headsel[:, o:o + 1].to_broadcast([NH, DH - 1])
                                      ).then_inc(dve_set, 1)
            dve.wait_ge(const_in, 96)
            nc.vector.tensor_tensor(w_gate[:, KD:2 * KD, :], w_gate[:, KD:2 * KD, :], w_gate[:, 2 * KD:3 * KD, :],
                                    ALU.add).then_inc(dve_set, 1)
            dve.wait_ge(act_set, 4)
            nc.vector.tensor_tensor(rw_lo[:, :, :], rw[:, :, :], rw_hi[:, :, :].bitcast(f32), ALU.subtract
                                    ).then_inc(dve_set, 1)
            dve.wait_ge(dve_set, 12)

            def ahead(part, b, j):
                c = b * CPB + j
                if part == 1:
                    dve.wait_ge(x_in[j], 16 * b + 16)
                    step(nc.vector.bn_stats(st1[:, 0, :], x[:, j, 0:512]))
                    step(nc.vector.bn_stats(st1[:, 1, :], x[:, j, 512:1024]))
                    chain.settle_apart(past)
                    link(nc.vector.bn_aggr(mv1[:, :], st1[:, :, :].rearrange("p a b -> p (a b)")))
                    nc.vector.tensor_scalar(rs1[:, 0:1], mv1[:, 1:2], LN_EPS, None, ALU.add).then_inc(var1, 1)
                    dve.wait_ge(rs1_rdy, c + 1)
                    ge(dve, gates_ps, c)
                    nc.vector.tensor_scalar(q[:, :, :].rearrange("p h d -> p (h d)"), x[:, j, :], mv1[:, 0:1], rs1[:, 1:2],
                                            ALU.subtract, ALU.mult).then_inc(q_rdy, 1)
                if part == 2:
                    dve.wait_ge(gates_ps, c + 1)
                    link(nc.vector.tensor_tensor(gates[:, :], p_gate[:, 0:2 * NH], gate_bias[:, :], ALU.add))
                    f = gates[:, NH:2 * NH]
                    nc.vector.scalar_tensor_tensor(out=absf[:, :], in0=f, scalar=-1.0, in1=f, op0=ALU.mult,
                                                   op1=ALU.max).then_inc(absf_rdy, 1)
                    dve.wait_ge(lnf_rdy, 2 * c + 2)
                    dve.wait_ge(absf_rdy, c + 1)
                    nc.vector.scalar_tensor_tensor(out=f, in0=f, scalar=0.0, in1=lnf[:, 1, :], op0=ALU.min,
                                                   op1=ALU.subtract).then_inc(lf_rdy, 1)
                    dve.wait_ge(gt_ps, c + 1)
                    ge(dve, cols_ps, c)
                    now, was = j % 2, (j + 1) % 2
                    f0 = 0.0 if j == 0 else fcum[:, was, P - 1:P]
                    g0 = NEG if j == 0 else gmax[:, was, P - 1:P]
                    link(nc.vector.tensor_tensor_scan(fcum[:, now, :], one_row[:, :], p_row[0:NH, P:2 * P], f0,
                                                      ALU.mult, ALU.add))
                    link(nc.vector.tensor_tensor(rows[:, 0, :], p_row[0:NH, 0:P], fcum[:, now, :], ALU.subtract))
                    link(nc.vector.tensor_tensor_scan(gmax[:, now, :], zero_row[:, :], rows[:, 0, :], g0,
                                                      ALU.add, ALU.max))
                    ge(dve, g_out, 16 * c)
                    nc.vector.tensor_scalar(neg_g[:, :], gmax[:, now, :], -1.0, None, ALU.mult).then_inc(neg_g_rdy, 1)
                    step(nc.vector.tensor_scalar(rows[:, 1, :], rows[:, 0, :], gmax[:, now, P - 1:P], None, ALU.subtract))
                    if 0 < j < CPB - 1:
                        step(nc.vector.tensor_tensor(dec[:, 0:1], gmax[:, was, P - 1:P], gmax[:, now, P - 1:P], ALU.subtract))
                    if j > 0:
                        dve.wait_ge(neg_g_rdy, c + 1)
                        step(nc.vector.tensor_scalar(rows[:, 3, :], neg_g[:, :], gmax[:, was, P - 1:P], None, ALU.add))
                    nc.vector.scalar_tensor_tensor(out=rows[:, 2, :], in0=fcum[:, now, :], scalar=-1.0,
                                                   in1=gmax[:, now, :], op0=ALU.mult, op1=ALU.subtract
                                                   ).then_inc(rows_rdy, 1)
                    if 0 < j < CPB - 1:
                        n = (CPB - 2) * b + j
                        dve.wait_ge(dec_rdy, n)
                        ge(dve, dec_ps, n - 1)
                        nc.vector.tensor_scalar(decm[:, :], headmask[:, :], dec[:, 1:2], None, ALU.mult).then_inc(decm_rdy, 1)
                if part == 3 and j > 0:
                    dve.wait_ge(cols_rdy, 2 * c + 2)
                    link(nc.vector.tensor_scalar(qfac[:, :], cols[:, j, 3, :], DH ** -0.5, None, ALU.mult))
                    nc.vector.tensor_tensor(qs[:, :, :], q[:, :, :], qfac[:, :, None].to_broadcast([P, NH, DH]),
                                            ALU.mult).then_inc(qs_rdy, 1)

            def mid(part, b, j):
                c = b * CPB + j
                if part == 1:
                    dve.wait_ge(d_rdy, NH * c + NH)
                for g in (2 * part - 2, 2 * part - 1):
                    dve.wait_ge(sc_ps, NG * c + g + 1)
                    ge(dve, u_ps, NG * c + g - 1)
                    nc.vector.scalar_tensor_tensor(
                        out=cmat[:, g % 2, :, :], in0=p_sc[:, :, :],
                        scalar=DH ** -0.5, in1=dmat[:, heads(g)[0]:heads(g)[-1] + 1:2, :],
                        op0=ALU.mult, op1=ALU.mult).then_inc(c_rdy, 1)
                if part == 2 and j < CPB - 1:
                    n = (CPB - 1) * b + j
                    if j > 0:
                        dve.wait_ge(dec_ps, (CPB - 2) * b + j)
                        dve.wait_ge(u_ps, NG * c + NG)
                        link(nc.vector.tensor_tensor(state[:, :, :], state[:, :, :],
                                                     p_gate[:, 64 + 64 * (j % 2):64 + 64 * (j % 2) + KD, None].to_broadcast([P, KD, HV]), ALU.mult))
                    for m in range(2):
                        half = state[:, 4 * m:4 * m + 4, :].rearrange("p j d -> p (j d)")
                        dve.wait_ge(ds_ps, 2 * n + m + 1)
                        if j > 0:
                            ins = nc.vector.tensor_tensor(half, half, p_u[m][:, 0:4 * HV], ALU.add)
                        else:
                            ins = nc.vector.tensor_copy(half, p_u[m][:, 0:4 * HV])
                        ins.then_inc(state_rdy, 1)

            def behind(part, b, j):
                c = b * CPB + j
                u = uc[:, j % 2, :, 0:DH]
                if part == 1:
                    dve.wait_ge(u_rdy, NG * c + NG)
                    den = uc[:, j % 2, :, DH]
                    link(nc.vector.scalar_tensor_tensor(out=nrm[:, 0, :], in0=den, scalar=-1.0, in1=den,
                                                        op0=ALU.mult, op1=ALU.max))
                    link(nc.vector.tensor_tensor(nrm[:, 0, :], nrm[:, 0, :], cols[:, j, 2, :], ALU.max))
                    link(nc.vector.tensor_scalar(nrm[:, 0, :], nrm[:, 0, :], H_EPS, None, ALU.add))
                    link(nc.vector.reciprocal(nrm[:, 1, :], nrm[:, 0, :]))
                    link(nc.vector.tensor_tensor(u, u, nrm[:, 1, :, None].to_broadcast([P, NH, DH]), ALU.mult))
                    link(nc.vector.tensor_reduce(out=mu[:, 0, :], in_=u, axis=AX.X, op=ALU.add))
                    link(nc.vector.tensor_scalar(mu[:, 1, :], mu[:, 0, :], 1.0 / DH, None, ALU.mult))
                    ge(dve, x1_rdy, c)
                    nc.vector.tensor_tensor(u, u, mu[:, 1, :, None].to_broadcast([P, NH, DH]), ALU.subtract
                                            ).then_inc(cen_rdy, 1)
                    dve.wait_ge(sq_rdy, c + 1)
                    link(nc.vector.tensor_reduce(out=var[:, 0, :], in_=sq[:, :, :], axis=AX.X, op=ALU.add))
                    nc.vector.tensor_scalar(var[:, 1, :], var[:, 0, :], 1.0 / DH, H_EPS, ALU.mult, ALU.add
                                            ).then_inc(var_rdy, 1)
                    dve.wait_ge(hrs_rdy, c + 1)
                    nc.vector.tensor_tensor(sq[:, :, :], u, var[:, 2, :, None].to_broadcast([P, NH, DH]), ALU.mult
                                            ).then_inc(o_rdy, 1)
                if part == 2:
                    dve.wait_ge(x1_rdy, c + 1)
                    step(nc.vector.bn_stats(st2[:, 0, :], x1[:, j % 2, 0:512]))
                    step(nc.vector.bn_stats(st2[:, 1, :], x1[:, j % 2, 512:1024]))
                    chain.settle_apart(past)
                    link(nc.vector.bn_aggr(mv2[:, :], st2[:, :, :].rearrange("p a b -> p (a b)")))
                    nc.vector.tensor_scalar(rs2[:, 0:1], mv2[:, 1:2], LN_EPS, None, ALU.add).then_inc(var2, 1)
                    dve.wait_ge(rs2_rdy, c + 1)
                    ge(dve, xn_out[j % 2], 16 * (2 * b + j // 2))
                    nc.vector.tensor_scalar(xn[:, j % 2, :], x1[:, j % 2, :], mv2[:, 0:1], rs2[:, 1:2],
                                            ALU.subtract, ALU.mult).then_inc(xn_rdy, 1)
                    for n in range(2):
                        dve.wait_ge(hi_rdy, 2 * c + n + 1)
                        nc.vector.tensor_tensor(xn_lo[:, 4 * n:4 * n + 4, :], p_tr[n][:, :, :],
                                                xn_hi[:, 4 * n:4 * n + 4, :].bitcast(f32), ALU.subtract).then_inc(lo_rdy, 1)
                    dve.wait_ge(lg_ps, c + 1)
                    step(nc.vector.tensor_copy(lg[:, :], p_rt[:, 0:NE]))
                    chain.settle_apart(past)
                    step(nc.vector.max(mx[:, :], lg[:, :]))
                    chain.settle_apart(past)
                    link(nc.vector.max_index(ix[:, :], mx[:, :], lg[:, :]))
                    nc.vector.tensor_tensor(ew[:, 0:1], mx[:, 1:2], mx[:, 0:1], ALU.subtract).then_inc(top_rdy, 1)
                    ecol = eidx[:, bass.ds(2 * c, 2)]
                    step(nc.vector.tensor_copy(ecol, ix[:, 0:2]))
                    link(nc.vector.tensor_copy(posf[:, :], ix[:, 0:2]))
                    for k in range(2):
                        step(nc.vector.tensor_scalar(hot[:, k, :], iota_e[:, :], posf[:, k:k + 1], None, ALU.is_equal))
                    settle()
                    nc.vector.tensor_tensor(hot[:, 2, :], hot[:, 0, :], hot[:, 1, :], ALU.add).then_inc(hot_rdy, 1)
                    dve.wait_ge(rank_ps, c + 1)
                    for k in range(2):
                        step(nc.vector.scalar_tensor_tensor(out=scr[:, k, :], in0=p_rt[:, 32:32 + NE], scalar=1.0,
                                                            in1=hot[:, k, :], op0=ALU.mult, op1=ALU.mult))
                    step(nc.vector.tensor_tensor(hot_acc[:, :], hot_acc[:, :], hot[:, 2, :], ALU.add))
                    settle()
                    link(nc.vector.tensor_reduce(out=rank[:, bass.ds(2 * c, 2)], in_=scr[:, :, :], axis=AX.X, op=ALU.add))
                    ge(dve, scat0, 16 * (c - 1))
                    ge(dve, scat1, 16 * (c - 1))
                    step(nc.vector.tensor_copy(tok[:, j % 2:j % 2 + 1], tok_all[:, bass.ds(c, 1)]))
                    nc.vector.scalar_tensor_tensor(out=posi[:, j % 2, :], in0=posf[:, :], scalar=float(CAP),
                                                   in1=rank[:, bass.ds(2 * c, 2)], op0=ALU.mult, op1=ALU.add
                                                   ).then_inc(pos_rdy, 1)
                    dve.wait_ge(ew_rdy, c + 1)
                    link(nc.vector.tensor_scalar(ew[:, 2:3], ew[:, 1:2], 1.0, None, ALU.add))
                    link(nc.vector.reciprocal(wts[:, bass.ds(2 * c, 1)], ew[:, 2:3]))
                    step(nc.vector.tensor_scalar(wts[:, bass.ds(2 * c + 1, 1)], ew[:, 1:2], wts[:, bass.ds(2 * c, 1)], None, ALU.mult))

            schedule(dve, chain, ahead, mid, behind, dve.Fori)
            settle()
            dve.wait_ge(rank_ps, NCH)
            dve.wait_ge(hot_rdy, NCH)

        @block.tensor
        def _(pe):
            pe.wait_ge(pool_set, 11)
            pe.wait_ge(dve_set, 12)

            def turn_tile(src, dst):
                for k in range(4):
                    last = nc.tensor.transpose(p_tr[dst][:, k, :], src[:, k * P:(k + 1) * P], ident[:, :])
                last.then_inc(tr_ps, 1)

            def p_tr_free(kind, b, j):
                copied, split = parted_by(kind, b, j, False)
                ge(pe, tr_sb, copied)
                ge(pe, lo_rdy, split)

            def ahead(part, b, j):
                c = b * CPB + j
                if part == 1:
                    pe.wait_ge(q_rdy, c + 1)
                    p_tr_free("q", b, j)
                    flat = q[:, :, :].rearrange("p h d -> p (h d)")
                    for n in range(2):
                        turn_tile(flat[:, 512 * n:512 * n + 512], n)
                    pe.wait_ge(ct_in[j], 16 * b + 16)
                    ge(pe, lf_rdy, c)
                    ge(pe, state_rdy, 2 * states_through(b, j, 2))
                    pe.wait_ge(tr_sb, parted_by("q", b, j, True)[0])
                    for k in range(2 * KD):
                        lhs = q_t[:, j % 2, k, :] if k < KD else ctx_t[:, j, k - KD, :]
                        last = nc.tensor.matmul(p_gate[:, 0:2 * NH], lhs, w_gate[:, k, :], start=(k == 0),
                                                stop=(k == 2 * KD - 1))
                    last.then_inc(gates_ps, 1)
                if part == 2:
                    pe.wait_ge(lf_rdy, c + 1)
                    ge(pe, cols_rdy, 2 * c)
                    for m in range(2):
                        last = nc.tensor.transpose(p_row[0:NH, m * P:(m + 1) * P], gates[:, m * NH:(m + 1) * NH], ident[:, :])
                    last.then_inc(gt_ps, 1)
                    ge_apart(pe, past, (rows_rdy, c + 1))
                    which = [r for r in range(4) if not (r == 1 and j == CPB - 1) and not (r == 3 and j == 0)]
                    for r in which:
                        last = nc.tensor.transpose(p_row[:, 256 + r * NH:256 + (r + 1) * NH], rows[:, r, :], ident[0:NH, 0:NH])
                    last.then_inc(cols_ps, 1)
                    if 0 < j < CPB - 1:
                        pe.wait_ge(decm_rdy, (CPB - 2) * b + j)
                        nc.tensor.matmul(p_gate[:, 64 + 64 * (j % 2):64 + 64 * (j % 2) + KD], headsel[:, :], decm[:, :], start=True, stop=True
                                         ).then_inc(dec_ps, 1)
                if part == 3 and j > 0:
                    pe.wait_ge(qs_rdy, (CPB - 1) * b + j)
                    p_tr_free("qs", b, j)
                    flat = qs[:, :, :].rearrange("p h d -> p (h d)")
                    for n in range(2):
                        turn_tile(flat[:, 512 * n:512 * n + 512], n)

            def scores(b, j, g):
                c = b * CPB + j
                ge(pe, c_rdy, NG * c + g)
                for n, h in enumerate(heads(g)):
                    lo = DH * (h % 2)
                    last = nc.tensor.matmul(p_sc[:, n, :], ctx_t[lo:lo + DH, j, h // 2, :],
                                            q_t[lo:lo + DH, j % 2, h // 2, :], start=True, stop=True)
                last.then_inc(sc_ps, 1)

            def values(b, j, g):
                c = b * CPB + j
                pe.wait_ge(c_rdy, NG * c + g + 1)
                ge(pe, u_rdy, NG * c + g - 1)
                if g < 2:
                    ge(pe, state_rdy, 2 * states_done(b, j))
                for n, h in enumerate(heads(g)):
                    lo = DH * (h % 2)
                    out = p_u[g % 2][:, n * HV:(n + 1) * HV]
                    last = nc.tensor.matmul(out, cmat[:, g % 2, n, :], ctx_v[:, j % 2, h, :], start=True, stop=(j == 0))
                    if j > 0:
                        last = nc.tensor.matmul(out, qs_t[lo:lo + DH, h // 2, :], state[lo:lo + DH, h // 2, :],
                                                start=False, stop=True)
                last.then_inc(u_ps, 1)

            def states_done(b, j):
                return (CPB - 1) * b + j

            def mid(part, b, j):
                c = b * CPB + j
                if part == 1:
                    if j > 0:
                        pe.wait_ge(tr_sb, parted_by("qs", b, j, True)[0])
                    pe.wait_ge(cv_in[j % 2], 16 * (2 * b + j // 2) + 16)
                    scores(b, j, 0)
                    scores(b, j, 1)
                    values(b, j, 0)
                if part == 2:
                    scores(b, j, 2)
                    values(b, j, 1)
                    scores(b, j, 3)
                    values(b, j, 2)
                    values(b, j, 3)
                    if j < CPB - 1:
                        pe.wait_ge(ks_rdy, states_done(b, j) + 1)
                        for m in range(2):
                            pe.wait_ge(u_rdy, NG * c + 3 + m)
                            for n in range(8):
                                h = 8 * m + n
                                lo = DH * (h % 2)
                                last = nc.tensor.matmul(p_u[m][lo:lo + DH, (n // 2) * HV:(n // 2 + 1) * HV],
                                                        ks[:, h, :], ctx_v[:, j % 2, h, :], start=True, stop=True)
                            last.then_inc(ds_ps, 1)

            def behind(part, b, j):
                c = b * CPB + j
                if part == 2:
                    pe.wait_ge(xn_rdy, c + 1)
                    p_tr_free("xn", b, j)
                    for n in range(2):
                        turn_tile(xn[:, j % 2, 512 * n:512 * n + 512], n)
                    pe.wait_ge(lo_rdy, 2 * c + 2)
                    ge(pe, pos_rdy, c)
                    trio = [(xn_hi, rw_hi), (xn_lo, rw_hi), (xn_hi, rw_lo)]
                    for k in range(KD):
                        for m, (a, w) in enumerate(trio):
                            last = nc.tensor.matmul(p_rt[:, 0:NE], a[:, k, :], w[:, k, :], start=(k == 0 and m == 0),
                                                    stop=(k == KD - 1 and m == 2))
                    last.then_inc(lg_ps, 1)
                    pe.wait_ge(hot_rdy, c + 1)
                    nc.tensor.matmul(p_rt[:, 32:32 + NE], upper[:, :], hot[:, 2, :], start=True, stop=False)
                    nc.tensor.matmul(p_rt[:, 32:32 + NE], ones[:, :], hot_acc[:, :], start=False, stop=True
                                     ).then_inc(rank_ps, 1)

            schedule(pe, None, ahead, mid, behind, pe.Fori)



def ffn_block(nc, t, keep, routed):
    f32, f32r, i32 = mybir.dt.float32, mybir.dt.float32r, mybir.dt.int32
    ACT, AX = mybir.ActivationFunctionType, mybir.AxisListType
    with ExitStack() as ctx:
        tag = "b" if routed else "a"

        def sb(name, shape, dt=f32):
            return ctx.enter_context(nc.sbuf_tensor(f"{name}_{tag}", shape, dt))

        def sem(name):
            return ctx.enter_context(nc.semaphore(f"{name}_{tag}"))

        ident, tgf = keep["ident"], keep["tgf"]
        stage = sb("stage", [P, PIECES, D])
        w_hi, w_lo = sb("w_hi", [P, PIECES, D], f32r), sb("w_lo", [P, PIECES, D], f32r)
        xg = sb("xg", [P, D])
        xt_hi, xt_lo = sb("xt_hi", [P, KD, P], f32r), sb("xt_lo", [P, KD, P], f32r)
        eg = sb("eg", [P, FE])
        h = sb("h", [P, FE])
        ht_hi, ht_lo = sb("ht_hi", [P, FE // P, P], f32r), sb("ht_lo", [P, FE // P, P], f32r)
        y = sb("y", [P, D])
        base_row = sb("base_row", [P, D])
        p_x = [ctx.enter_context(nc.psum_tensor(f"p_x{n}_{tag}", [P, 4, P], f32)) for n in range(2)]
        p_g = ctx.enter_context(nc.psum_tensor(f"p_g_{tag}", [P, FE], f32))
        p_up = ctx.enter_context(nc.psum_tensor(f"p_up_{tag}", [P, FE], f32))
        p_h = ctx.enter_context(nc.psum_tensor(f"p_h_{tag}", [P, FE // P, P], f32))
        p_y = [ctx.enter_context(nc.psum_tensor(f"p_y{n}_{tag}", [P, 512], f32)) for n in range(2)]
        if routed:
            r0, r1 = sb("r0", [P, D]), sb("r1", [P, D])
            idx = sb("idx", [P, 1], i32)
            cnt_i = sb("cnt_i", [P, NE], i32)
            cnt_f = sb("cnt_f", [P, 2, NE])
            one_e = sb("one_e", [P, NE])
            starts = sb("starts", [P, NE + 1])
            starts_i = sb("starts_i", [P, 3, NE + 1], i32)
            hot = sb("hot", [P, 2 * NCH, NE])
            slot_f, slot_i = sb("slot_f", [P, 2 * NCH]), sb("slot_i", [P, 2 * NCH], i32)
            ones = sb("ones", [P, P])

        past = sem("past")
        wg_in, wu_in, wd_in = sem("wg_in"), sem("wu_in"), sem("wd_in")
        x_in, idx_in, base_in, y_out, z_out, r0_in, r1_in = (
            sem("x_in"), sem("idx_in"), sem("base_in"), sem("y_out"), sem("z_out"), sem("r0_in"), sem("r1_in"))
        gu_hi, gu_split, d_hi, d_split, own_hi = (
            sem("gu_hi"), sem("gu_split"), sem("d_hi"), sem("d_split"), sem("own_hi"))
        xt_ps, xt_hi_rdy, xt_rdy = sem("xt_ps"), sem("xt_hi_rdy"), sem("xt_rdy")
        gu_ps, exp_rdy, silu_step, h_rdy = sem("gu_ps"), sem("exp_rdy"), sem("silu_step"), sem("h_rdy")
        ht_ps, ht_hi_rdy, ht_rdy = sem("ht_ps"), sem("ht_hi_rdy"), sem("ht_rdy")
        y_ps, y_rdy, join_step, z_rdy = sem("y_ps"), sem("y_rdy"), sem("join_step"), sem("z_rdy")
        if routed:
            fill_in = sem("fill_in")
            slot_now = sb("slot_now", [P, 2], i32)
            tab_step, tab_rdy, slots_rdy, slot_step = sem("tab_step"), sem("tab_rdy"), sem("slots_rdy"), sem("slot_step")
            cnt_go, cnt_ps = sem("cnt_go"), sem("cnt_ps")

        shared_e = NE if routed else 0

        def tiles(eng, body, finish):
            if not routed:
                body(0, None, 0, 0, True, None, False)
                body(1, 0, 0, 1, False, "shared", False)
                with eng.Fori(2, NCH - 1) as i:
                    body(i, i - 1, 0, i, False, "shared", False)
                body(NCH - 1, NCH - 2, 0, NCH - 1, False, "shared", True)
                finish(NCH, NCH - 1, 0, NCH)
                return
            eng.wait_ge(tab_rdy, 1)
            body(0, None, 0, None, True, None, False)
            body(1, 0, 0, None, False, "routed", False)
            with eng.Fori(2, start(eng, 1)) as i:
                body(i, i - 1, 0, None, False, "routed", False)
            with eng.Fori(1, NE) as e:
                begin, end = start(eng, e), start(eng, e + 1)
                body(begin, start(eng, e, 1), e, None, True, "routed", False)
                with eng.Fori(begin + 1, end) as i:
                    body(i, i - 1, e, None, False, "routed", False)
            n = start(eng, NE)
            body(n, start(eng, NE, 1), NE, 0, True, "routed", False)
            body(n + 1, n, NE, 1, False, "shared", False)
            with eng.Fori(2, NCH - 1) as c:
                body(n + c, n + (c - 1), NE, c, False, "shared", False)
            body(n + (NCH - 1), n + (NCH - 2), NE, NCH - 1, False, "shared", True)
            finish(n + NCH, n + (NCH - 1), NE, NCH)

        def start(eng, e, less=0):
            return eng.value_load(starts_i[0:1, less, bass.ds(e, 1)], min_val=MIN_TILES - less, max_val=MAX_TILES - less)

        xn_rows = t["xn"].rearrange("(c p) d -> c p d", p=P)
        base_rows = (t["z"] if routed else t["x1"]).rearrange("(c p) d -> c p d", p=P)
        z_rows = (t["out"] if routed else t["z"]).rearrange("(c p) d -> c p d", p=P)

        block = ctx.enter_context(nc.Block())

        @block.sync
        def _(sp):
            def load_weights(e, shared):
                if shared:
                    cols = slice(FE, 2 * FE) if routed else slice(0, FE)
                    gate, up = t["sg"][:, cols], t["su"][:, cols]
                    down = t["sd"][cols, :]
                else:
                    gate, up, down = (t[n][bass.ds(e, 1)].rearrange("o a b -> (o a) b") for n in ("eg", "eu", "ed"))
                ge(sp, gu_split, GUP * e)
                sp.dma_start(stage[:, 0:GUP, 0:FE], gate.rearrange("(k p) f -> p k f", p=P)).then_inc(wg_in, 16)
                sp.dma_start(stage[:, 0:GUP, FE:D], up.rearrange("(k p) f -> p k f", p=P)).then_inc(wu_in, 16)
                ge(sp, d_split, (PIECES - GUP) * e)
                sp.dma_start(stage[:, GUP:PIECES, :], down.rearrange("(k p) f -> p k f", p=P)).then_inc(wd_in, 16)

            def store_routed(q):
                sp.wait_ge(y_rdy, 2 * q + 2)
                sp.dma_start(t["y"][bass.ds(q * P, P), :], y[:, :]).then_inc(y_out, 16)

            def load_base(c):
                ge(sp, z_rdy, c)
                sp.dma_start(base_row[:, :], base_rows[c]).then_inc(base_in, 16)

            def store_joined(c):
                sp.wait_ge(z_rdy, c)
                sp.dma_start(z_rows[c - 1], y[:, :]).then_inc(z_out, 16)

            load_weights(0, not routed)
            if routed:
                sp.wait_ge(tab_rdy, 1)
                load_weights(1, False)
                with sp.Fori(start(sp, NE), MAX_TILES) as f:
                    sp.dma_start(t["y"][bass.ds(f * P, P), :], base_rows[0]).then_inc(fill_in, 16)
                store_routed(0)
                with sp.Fori(2, start(sp, 1)) as i:
                    store_routed(i - 1)
                with sp.Fori(1, NE - 1) as e:
                    store_routed(start(sp, e, 1))
                    load_weights(e + 1, False)
                    with sp.Fori(start(sp, e) + 1, start(sp, e + 1)) as i:
                        store_routed(i - 1)
                store_routed(start(sp, NE - 1, 1))
                load_weights(NE, True)
                with sp.Fori(start(sp, NE - 1) + 1, start(sp, NE)) as i:
                    store_routed(i - 1)
                store_routed(start(sp, NE, 1))
            load_base(0)
            with sp.Fori(1, NCH) as c:
                load_base(c)
                store_joined(c)
            store_joined(NCH)
            sp.wait_ge(z_out, 16 * NCH)

        @block.gpsimd
        def _(pool):
            def rows_of(i, e, c, first):
                if c is None:
                    part = e * (CAP // P)
                    if not first:
                        part = nc.s_assert_within(
                            part + (i - first_tile[0]), 0, NE * CAP // P,
                            skip_runtime_bounds_check_because="an expert has CAP // P tiles at most")
                    ge_apart(pool, past, (x_in, 16 * i))
                    pool.dma_start(idx[:, :], list_parts[bass.ds(part, 1)].rearrange("o p w -> (o p) w")
                                   ).then_inc(idx_in, 16)
                ge_apart(pool, past, (idx_in, 16 * i + 16 if c is None else 0), (xt_ps, i))
                if c is None:
                    nc.gpsimd.indirect_dma_start(
                        out=xg[:, :], out_offset=None, in_=t["xn"],
                        in_offset=bass.IndirectOffsetOnAxis(ap=idx[:, :], axis=0)).then_inc(x_in, 16)
                else:
                    pool.dma_start(xg[:, :], xn_rows[c]).then_inc(x_in, 16)

            first_tile = [0]
            list_parts = t["lists"].rearrange("(n p) w -> n p w", p=P)

            def body(i, q, e, c, first, prev, last):
                if first:
                    first_tile[0] = i
                rows_of(i, e, c, first)
                if prev == "shared" and routed:
                    gather(c - 1, c)

            def gather(k, c):
                if isinstance(c, int) and c == 1:
                    own = start(pool, NE)
                    filled = pool.value_load(starts_i[0:1, 2, NE:NE + 1], min_val=1, max_val=MAX_TILES)
                    pool.wait_ge(y_out, 16 * own)
                    pool.wait_ge(fill_in, 16 * filled)
                    pool.wait_ge(slots_rdy, 1)
                ge_apart(pool, past, (z_rdy, k))
                for m in range(2):
                    nc.gpsimd.tensor_copy(slot_now[:, m:m + 1], slot_i[:, bass.ds(2 * k + m, 1)]).then_inc(slot_step, 1)
                ge_apart(pool, past, (slot_step, 2 * c))
                for m, (r, done) in enumerate(((r0, r0_in), (r1, r1_in))):
                    nc.gpsimd.indirect_dma_start(
                        out=r[:, :], out_offset=None, in_=t["y"],
                        in_offset=bass.IndirectOffsetOnAxis(ap=slot_now[:, m:m + 1], axis=0)).then_inc(done, 16)

            def finish(i, q, e, c):
                if routed:
                    gather(c - 1, c)

            tiles(pool, body, finish)

        @block.scalar
        def _(act):
            def split_gu(i, e):
                act.wait_ge(wg_in, 16 * e + 16)
                act.wait_ge(wu_in, 16 * e + 16)
                ge(act, gu_ps, i)
                for p in range(DVE_HI, GUP):
                    nc.scalar.activation(w_hi[:, p, :], stage[:, p, :], ACT.Copy).then_inc(gu_hi, 1)

            def split_d(i, e, prev):
                act.wait_ge(wd_in, 16 * e + 16)
                if prev:
                    act.wait_ge(y_ps, 2 * i)
                for p in range(GUP, PIECES):
                    nc.scalar.activation(w_hi[:, p, :], stage[:, p, :], ACT.Copy).then_inc(d_hi, 1)

            def h_high(i):
                act.wait_ge(ht_ps, i)
                nc.scalar.activation(ht_hi[:, :, :], p_h[:, :, :], ACT.Copy).then_inc(ht_hi_rdy, 1)

            def x_high(i):
                act.wait_ge(xt_ps, i + 1)
                for n in range(2):
                    nc.scalar.activation(xt_hi[:, 4 * n:4 * n + 4, :], p_x[n][:, :, :], ACT.Copy).then_inc(xt_hi_rdy, 1)

            def y_copy(q):
                ge(act, y_out, 16 * q)
                for n in range(2):
                    act.wait_ge(y_ps, 2 * q + (n + 1))
                    nc.scalar.activation(y[:, 512 * n:512 * n + 512], p_y[n][:, :], ACT.Copy).then_inc(y_rdy, 1)

            def body(i, q, e, c, first, prev, last):
                if first:
                    split_gu(i, e)
                if prev:
                    h_high(i)
                act.wait_ge(gu_ps, i + 1)
                nc.scalar.activation(eg[:, :], p_g[:, :], ACT.Exp, scale=-1.0).then_inc(exp_rdy, 1)
                if not last:
                    x_high(i + 1)
                if prev == "routed":
                    y_copy(q)
                if first:
                    split_d(i, e, prev)

            x_high(0)
            tiles(act, body, lambda i, q, e, c: h_high(i))

        @block.vector
        def _(dve):
            def split(p, sem_hi, n_hi, sem_lo):
                dve.wait_ge(sem_hi, n_hi)
                nc.vector.tensor_tensor(w_lo[:, p, :], stage[:, p, :], w_hi[:, p, :].bitcast(f32), ALU.subtract
                                        ).then_inc(sem_lo, 1)

            def split_gu(i, e):
                dve.wait_ge(wg_in, 16 * e + 16)
                dve.wait_ge(wu_in, 16 * e + 16)
                ge(dve, gu_ps, i)
                for p in range(DVE_HI):
                    nc.vector.tensor_copy(w_hi[:, p, :], stage[:, p, :]).then_inc(own_hi, 1)
                    split(p, own_hi, DVE_HI * e + p + 1, gu_split)
                for p in range(DVE_HI, GUP):
                    split(p, gu_hi, (GUP - DVE_HI) * e + (p - DVE_HI + 1), gu_split)

            def split_d(e):
                for p in range(GUP, PIECES):
                    split(p, d_hi, (PIECES - GUP) * e + (p - GUP + 1), d_split)

            def h_low(i):
                dve.wait_ge(ht_hi_rdy, i)
                nc.vector.tensor_tensor(ht_lo[:, :, :], p_h[:, :, :], ht_hi[:, :, :].bitcast(f32), ALU.subtract
                                        ).then_inc(ht_rdy, 1)

            def x_low(i):
                for n in range(2):
                    dve.wait_ge(xt_hi_rdy, 2 * i + (n + 1))
                    nc.vector.tensor_tensor(xt_lo[:, 4 * n:4 * n + 4, :], p_x[n][:, :, :],
                                            xt_hi[:, 4 * n:4 * n + 4, :].bitcast(f32), ALU.subtract).then_inc(xt_rdy, 1)

            def silu(i):
                dve.wait_ge(exp_rdy, i + 1)
                nc.vector.tensor_scalar(eg[:, :], eg[:, :], 1.0, None, ALU.add).then_inc(silu_step, 1)
                dve.wait_ge(silu_step, 3 * i + 1)
                nc.vector.reciprocal(eg[:, :], eg[:, :]).then_inc(silu_step, 1)
                dve.wait_ge(silu_step, 3 * i + 2)
                nc.vector.tensor_tensor(h[:, :], p_g[:, :], eg[:, :], ALU.mult).then_inc(silu_step, 1)
                dve.wait_ge(silu_step, 3 * i + 3)
                nc.vector.tensor_tensor(h[:, :], h[:, :], p_up[:, :], ALU.mult).then_inc(h_rdy, 1)

            def join(q, c):
                k = c - 1
                dve.wait_ge(base_in, 16 * c)
                if routed:
                    dve.wait_ge(r0_in, 16 * c)
                    nc.vector.tensor_scalar(r0[:, :], r0[:, :], keep["wts"][:, bass.ds(2 * k, 1)], None, ALU.mult
                                            ).then_inc(join_step, 1)
                    dve.wait_ge(r1_in, 16 * c)
                    dve.wait_ge(join_step, 4 * k + 1)
                    nc.vector.scalar_tensor_tensor(out=r0[:, :], in0=r1[:, :], scalar=keep["wts"][:, bass.ds(2 * k + 1, 1)],
                                                   in1=r0[:, :], op0=ALU.mult, op1=ALU.add).then_inc(join_step, 1)
                    dve.wait_ge(join_step, 4 * k + 2)
                    if isinstance(c, int) and c == 1:
                        dve.wait_ge(y_out, 16 * q)
                ge(dve, z_out, 16 * k)
                for n in range(2):
                    half = slice(512 * n, 512 * n + 512)
                    dve.wait_ge(y_ps, 2 * q + (n + 1))
                    src = p_y[n][:, :]
                    if routed:
                        nc.vector.tensor_tensor(r0[:, half], p_y[n][:, :], r0[:, half], ALU.add).then_inc(join_step, 1)
                        dve.wait_ge(join_step, 4 * k + n + 3)
                        src = r0[:, half]
                    last = nc.vector.scalar_tensor_tensor(out=y[:, half], in0=src, scalar=tgf[:, 0:1],
                                                          in1=base_row[:, half], op0=ALU.mult, op1=ALU.add)
                last.then_inc(z_rdy, 1)

            def tables():
                steps = [0]

                def link(ins):
                    ins.then_inc(tab_step, 1)
                    steps[0] += 1
                    dve.wait_ge(tab_step, steps[0])

                link(nc.vector.memset(ones[:, :], 1.0))
                link(nc.vector.memset(one_e[:, :], 1.0))
                link(nc.vector.memset(starts[:, 0:1], 0.0))
                nc.vector.memset(xg[:, 0:1], 0.0).then_inc(cnt_go, 1)
                dve.wait_ge(cnt_ps, 1)
                link(nc.vector.tensor_scalar(cnt_i[:, :], p_y[0][:, 0:NE], float(P - 1), None, ALU.add))
                link(nc.vector.tensor_scalar(cnt_i[:, :], cnt_i[:, :], 7, None, ALU.arith_shift_right))
                link(nc.vector.tensor_scalar(cnt_f[:, 0, :], cnt_i[:, :], float(MIN_TILES), None, ALU.max))
                link(nc.vector.tensor_scalar(cnt_f[:, 0, 0:1], cnt_f[:, 0, 0:1], float(MIN_TILES + 1), None, ALU.max))
                link(nc.vector.tensor_tensor_scan(starts[:, 1:NE + 1], one_e[:, :], cnt_f[:, 0, :], 0.0, ALU.mult, ALU.add))
                link(nc.vector.tensor_copy(starts_i[:, 0, :], starts[:, :]))
                link(nc.vector.tensor_scalar(starts_i[:, 1, :], starts[:, :], -1.0, None, ALU.add))
                link(nc.vector.tensor_scalar(starts_i[:, 2, :], starts[:, :], -1.0, float(MAX_TILES), ALU.mult, ALU.add))
                nc.vector.memset(xg[:, 0:1], 0.0).then_inc(tab_rdy, 1)
                link(nc.vector.tensor_scalar(cnt_f[:, 1, :], starts[:, 0:NE], float(P), None, ALU.mult))
                link(nc.vector.tensor_tensor(hot[:, :, :], keep["iota_e"][:, None, :].to_broadcast([P, 2 * NCH, NE]),
                                             keep["eidx"][:, :, None].to_broadcast([P, 2 * NCH, NE]), ALU.is_equal))
                link(nc.vector.tensor_tensor(hot[:, :, :], hot[:, :, :],
                                             cnt_f[:, 1, None, :].to_broadcast([P, 2 * NCH, NE]), ALU.mult))
                link(nc.vector.tensor_reduce(out=slot_f[:, :], in_=hot[:, :, :], axis=AX.X, op=ALU.add))
                nc.vector.tensor_tensor(slot_i[:, :], slot_f[:, :], keep["rank"][:, :], ALU.add).then_inc(slots_rdy, 1)

            def body(i, q, e, c, first, prev, last):
                if first:
                    split_gu(i, e)
                if prev:
                    h_low(i)
                silu(i)
                if not last:
                    x_low(i + 1)
                if prev == "shared":
                    join(q, c)
                if first:
                    split_d(e)

            def finish(i, q, e, c):
                h_low(i)
                join(q, c)

            if routed:
                tables()
            x_low(0)
            tiles(dve, body, finish)

        @block.tensor
        def _(pe):
            trio = ((xt_hi, w_hi), (xt_lo, w_hi), (xt_hi, w_lo))

            def turn_x(i):
                pe.wait_ge(x_in, 16 * i + 16)
                for k in range(KD):
                    last = nc.tensor.transpose(p_x[k // 4][:, k % 4, :], xg[:, k * P:(k + 1) * P], ident[:, :])
                last.then_inc(xt_ps, 1)

            def turn_h(i):
                pe.wait_ge(h_rdy, i)
                for k in range(FE // P):
                    last = nc.tensor.transpose(p_h[:, k, :], h[:, k * P:(k + 1) * P], ident[:, :])
                last.then_inc(ht_ps, 1)

            def down(i, e):
                pe.wait_ge(ht_rdy, i)
                for n in range(2):
                    for k in range(FE // P):
                        if n == 0:
                            pe.wait_ge(d_split, (PIECES - GUP) * e + (k + 1))
                        w = slice(512 * n, 512 * n + 512)
                        for m, (a, b) in enumerate(((ht_hi, w_hi), (ht_lo, w_hi), (ht_hi, w_lo))):
                            last = nc.tensor.matmul(p_y[n][:, :], a[:, k, :], b[:, GUP + k, w],
                                                    start=(k == 0 and m == 0), stop=(k == FE // P - 1 and m == 2))
                    last.then_inc(y_ps, 1)

            def body(i, q, e, c, first, prev, last):
                ge(pe, h_rdy, i)
                for k in range(KD):
                    if k % 4 == 0:
                        pe.wait_ge(xt_rdy, 2 * i + (k // 4 + 1))
                    pe.wait_ge(gu_split, GUP * e + (k + 1))
                    for m, (a, w) in enumerate(trio):
                        for out, o in ((p_g, 0), (p_up, FE)):
                            mm = nc.tensor.matmul(out[:, :], a[:, k, :], w[:, k, o:o + FE],
                                                  start=(k == 0 and m == 0), stop=(k == KD - 1 and m == 2))
                    if k == 3 and prev:
                        turn_h(i)
                mm.then_inc(gu_ps, 1)
                if not last:
                    turn_x(i + 1)
                if prev:
                    down(i, e - 1 if first else e)

            def finish(i, q, e, c):
                turn_h(i)
                down(i, e)

            if routed:
                pe.wait_ge(cnt_go, 1)
                nc.tensor.matmul(p_y[0][:, 0:NE], ones[:, :], keep["hot_acc"][:, :], start=True, stop=True).then_inc(cnt_ps, 1)
            turn_x(0)
            tiles(pe, body, finish)


def build(nc, t):
    f32 = mybir.dt.float32
    with ExitStack() as ctx:
        shapes = {"ident": [P, P], "iota_e": [P, NE], "hot_acc": [P, NE], "tgf": [P, 1],
                  "eidx": [P, 2 * NCH], "rank": [P, 2 * NCH], "wts": [P, 2 * NCH]}
        keep = {n: ctx.enter_context(nc.sbuf_tensor(n, s, f32)) for n, s in shapes.items()}
        mix_block(nc, t, keep)
        ffn_block(nc, t, keep, False)
        ffn_block(nc, t, keep, True)


def kernel(**inputs):
    import numpy as _np
    import concourse.bacc as _bacc
    from concourse import mybir as _mybir
    from concourse.bass_utils import run_bass_kernel_spmd as _run

    a = {k: _np.asarray(v) for k, v in inputs.items()}
    ctx = a["ctx_2048"].reshape(T, D)
    given = {
        "x": a["x"].reshape(T, D),
        "ctx": ctx,
        "ctx_t": ctx.reshape(NCH, P, KD, P).transpose(0, 3, 2, 1),
        "w_gate": _np.concatenate([a["L0_xattn_Wi"], a["L0_xattn_Wf"]], axis=1),
        "gate_bias": _np.concatenate([a["L0_xattn_bi"], a["L0_xattn_bf"]]),
        "rw": a["L0_ffn_router_w"].T,
        "ln_scale": a["L0_xattn_ln_scale"],
        "g_xattn": a["g_xattn"].reshape(1),
        "g_ffn": a["g_ffn"].reshape(1),
        "eg": a["L0_ffn_gate_w"],
        "eu": a["L0_ffn_up_w"],
        "ed": a["L0_ffn_down_w"],
        "sg": a["L0_ffn_shared_gate_w"],
        "su": a["L0_ffn_shared_up_w"],
        "sd": a["L0_ffn_shared_down_w"],
    }
    nc = _bacc.Bacc("TRN2", target_bir_lowering=False, num_devices=1)
    f32, i32 = _mybir.dt.float32, _mybir.dt.int32
    arrays, t = {}, {}
    for name, value in given.items():
        value = _np.ascontiguousarray(value)
        arrays[f"in_{name}"] = value
        t[name] = nc.dram_tensor(f"in_{name}", value.shape, _mybir.dt.from_np(value.dtype), kind="ExternalInput").ap()
    for name, shape, dt in (("x1", (T, D), f32), ("xn", (T, D), f32), ("z", (T, D), f32), ("g_row", (NH, P), f32),
                            ("lists", (NE * CAP + P, 1), i32), ("y", (MAX_TILES * P, D), f32)):
        t[name] = nc.dram_tensor(f"mid_{name}", shape, dt, kind="Internal").ap()
    out = nc.dram_tensor("out_0", (T, D), f32, kind="ExternalOutput").ap()
    t["out"] = out
    build(nc, t)
    r = _run(nc, [arrays], core_ids=[0])
    return r.results[0]["out_0"].reshape(B, S, D)
```

```python
from contextlib import ExitStack

import numpy as np

import concourse.bass as bass
from concourse import mybir
from concourse.alu_op_type import AluOpType as ALU

P = 128
B, S, D = 8, 512, 1024
T = B * S
NH, DH = 16, 64
NE, FE, FS = 16, 512, 1024
KD = D // P
NCH = T // P
CPB = S // P
HV = DH + 1
HG = 4
NG = NH // HG
LN_EPS, H_EPS = 1e-5, 1e-6
MIN_TILES = 2
MAX_TILES = 2 * T // P + MIN_TILES * NE + 2
CAP = T
PIECES = 12
GUP = 8
DVE_HI = 2
NEG = -3.0e38
DVE_PER_BATCH = 146


def ge(eng, sem, n):
    if isinstance(n, int) and n <= 0:
        return
    eng.wait_ge(sem, n)


def ge_apart(eng, past, *waits):
    for sem, n in waits:
        ge(eng, sem, n)
    eng.sem_inc(past, 1)


class Chain:

    def __init__(self, eng, sem):
        self.eng, self.sem, self.base, self.n = eng, sem, 0, 0

    def step(self, ins):
        ins.then_inc(self.sem, 1)
        self.n += 1

    def settle(self):
        self.eng.wait_ge(self.sem, self.base + self.n)

    def settle_apart(self, past):
        ge_apart(self.eng, past, (self.sem, self.base + self.n))

    def link(self, ins):
        self.step(ins)
        self.settle()


def mix_block(nc, t, keep):
    f32, f32r, i32, u32 = mybir.dt.float32, mybir.dt.float32r, mybir.dt.int32, mybir.dt.uint32
    ACT, AX = mybir.ActivationFunctionType, mybir.AxisListType
    with ExitStack() as ctx:
        def sb(name, shape, dt=f32):
            return ctx.enter_context(nc.sbuf_tensor(name, shape, dt))

        def pb(name, shape, dt=f32):
            return ctx.enter_context(nc.psum_tensor(name, shape, dt))

        def sem(name):
            return ctx.enter_context(nc.semaphore(name))

        ident = keep["ident"]
        upper = sb("upper", [P, P])
        ones = sb("ones", [P, P])
        headsel = sb("headsel", [NH, P])
        headmask = sb("headmask", [NH, KD])
        one_row = sb("one_row", [NH, P])
        zero_row = sb("zero_row", [NH, P])
        w_gate = sb("w_gate", [P, 3 * KD, 2 * NH])
        gate_bias = sb("gate_bias", [P, 2 * NH])
        rw = sb("rw", [P, KD, NE])
        lns = sb("lns", [P, D])
        gx = sb("gx", [P, 2])
        iota_e = keep["iota_e"]
        tok_all = sb("tok_all", [P, NCH], i32)
        zero_i = sb("zero_i", [P, (NE * CAP + P) // P], i32)
        mhalf = sb("mhalf", [P, NH])
        x = sb("x", [P, 4, D])
        ctx_t = sb("ctx_t", [P, 4, KD, P])
        ctx_v = sb("ctx_v", [P, 2, NH, HV])
        q = sb("q", [P, NH, DH])
        q_t = sb("q_t", [P, 2, KD, P])
        qs = sb("qs", [P, NH, DH])
        qs_t = sb("qs_t", [P, KD, P])
        gb = sb("gb", [P, NH, P])
        dmat = sb("dmat", [P, 2, NH, P])
        ks = sb("ks", [P, NH, DH])
        cmat = sb("cmat", [P, 2, HG, P])
        uc = sb("uc", [P, 2, NH, HV])
        state = sb("state", [P, KD, HV])
        sq = sb("sq", [P, NH, DH])
        x1 = sb("x1", [P, 2, D])
        xn = sb("xn", [P, 2, D])
        xn_t = sb("xn_t", [P, KD, P])
        st1, mv1, rs1 = sb("st1", [P, 2, 6]), sb("mv1", [P, 2]), sb("rs1", [P, 2])
        st2, mv2, rs2 = sb("st2", [P, 2, 6]), sb("mv2", [P, 2]), sb("rs2", [P, 2])
        gates = sb("gates", [P, 2 * NH])
        absf, lnf = sb("absf", [P, NH]), sb("lnf", [P, 2, NH])
        fcum = sb("fcum", [NH, 2, P])
        gmax = sb("gmax", [NH, 2, P])
        rows = sb("rows", [NH, 4, P])
        neg_g = sb("neg_g", [NH, P])
        dec = sb("dec", [NH, 2])
        decm = sb("decm", [NH, KD])
        cols = sb("cols", [P, 4, 4, NH])
        qfac = sb("qfac", [P, NH])
        nrm, mu, var = sb("nrm", [P, 2, NH]), sb("mu", [P, 2, NH]), sb("var", [P, 3, NH])
        lg, mx, ix = sb("lg", [P, NE]), sb("mx", [P, 8]), sb("ix", [P, 8], u32)
        hot = sb("hot", [P, 3, NE])
        hot_acc = keep["hot_acc"]
        scr = sb("scr", [P, 2, NE])
        posf, posi = sb("posf", [P, 2]), sb("posi", [P, 2, 2], i32)
        tok = sb("tok", [P, 2], i32)
        ew = sb("ew", [P, 3])
        eidx, rank, wts = keep["eidx"], keep["rank"], keep["wts"]
        p_tr = [pb(f"p_tr{n}", [P, 4, P]) for n in range(2)]
        p_sc = pb("p_sc", [P, HG, P])
        p_u = [pb(f"p_u{n}", [P, 512]) for n in range(2)]
        p_gate = pb("p_gate", [P, 512])
        p_row = pb("p_row", [P, 512])
        p_rt = pb("p_rt", [P, 512])

        past = sem("past")
        stage_in = [sem(f"stage_in{n}") for n in range(3)]
        const_in, table_in, scat0, scat1 = sem("const_in"), sem("table_in"), sem("scat0"), sem("scat1")
        x_in = [sem(f"x_in{n}") for n in range(4)]
        ct_in = [sem(f"ct_in{n}") for n in range(4)]
        cv_in = [sem(f"cv_in{n}") for n in range(2)]
        g_out, gb_in = sem("g_out"), sem("gb_in")
        x1_out = [sem(f"x1_out{n}") for n in range(2)]
        xn_out = [sem(f"xn_out{n}") for n in range(2)]
        pool_set, dve_set, act_set = sem("pool_set"), sem("dve_set"), sem("act_set")
        dve_steps, scaled_rdy = sem("dve_steps"), sem("scaled_rdy")
        var1, rs1_rdy, q_rdy = sem("var1"), sem("rs1_rdy"), sem("q_rdy")
        tr_ps, tr_sb = sem("tr_ps"), sem("tr_sb")
        gates_ps, absf_rdy, lnf_rdy, lf_rdy = sem("gates_ps"), sem("absf_rdy"), sem("lnf_rdy"), sem("lf_rdy")
        gt_ps, neg_g_rdy, rows_rdy, cols_ps, cols_rdy = (sem("gt_ps"), sem("neg_g_rdy"), sem("rows_rdy"),
                                                         sem("cols_ps"), sem("cols_rdy"))
        dec_rdy, decm_rdy, dec_ps = sem("dec_rdy"), sem("decm_rdy"), sem("dec_ps")
        qs_rdy, gb_rdy, d_rdy, ks_rdy = sem("qs_rdy"), sem("gb_rdy"), sem("d_rdy"), sem("ks_rdy")
        sc_ps, c_rdy, u_ps, u_rdy, ds_ps, state_rdy = (
            sem("sc_ps"), sem("c_rdy"), sem("u_ps"), sem("u_rdy"), sem("ds_ps"), sem("state_rdy"))
        cen_rdy, sq_rdy, var_rdy, hrs_rdy, o_rdy, x1_rdy = (
            sem("cen_rdy"), sem("sq_rdy"), sem("var_rdy"), sem("hrs_rdy"), sem("o_rdy"), sem("x1_rdy"))
        var2, rs2_rdy, xn_rdy = sem("var2"), sem("rs2_rdy"), sem("xn_rdy")
        lg_ps, hot_rdy, rank_ps, pos_rdy = sem("lg_ps"), sem("hot_rdy"), sem("rank_ps"), sem("pos_rdy")
        top_rdy, ew_rdy = sem("top_rdy"), sem("ew_rdy")

        x_rows = t["x"].rearrange("(c p) d -> c p d", p=P)
        ctx_rows = t["ctx"].rearrange("(c p) (h d) -> c p h d", p=P, h=NH)
        x1_rows = t["x1"].rearrange("(c p) d -> c p d", p=P)
        xn_rows = t["xn"].rearrange("(c p) d -> c p d", p=P)

        TURN = ("A1", "A2", "B0", "D1", "B1", "A3", "E1", "B2", "A4", "B3", "A5",
                "E2", "A6", "C1", "E3", "B4", "A7", "C2", "L1", "E4", "A8")
        OFFSET = {"L": 2, "A": 1, "B": 0, "C": -1, "D": -2, "E": -2}

        def schedule(eng, chain, stages, fori):
            def turn(b, j):
                for stage, part in TURN:
                    at = j + OFFSET[stage]
                    where = (b + at // CPB, at % CPB) if at // CPB else (b, at)
                    if isinstance(where[0], int) and not 0 <= where[0] < B:
                        continue
                    if stage in stages:
                        stages[stage](int(part), *where)

            for stage, part, j in [("L", 1, 0)] + [("A", part, 0) for part in range(1, 9)] + [("L", 1, 1)]:
                if stage in stages:
                    stages[stage](part, 0, j)
            for j in range(CPB):
                turn(0, j)
            before = chain.n if chain else 0
            with fori(1, B - 1) as b:
                if chain:
                    chain.base = (b - 1) * chain.per
                for j in range(CPB):
                    turn(b, j)
                if chain:
                    assert chain.n - before == chain.per, (chain.n - before, chain.per)
            if chain:
                chain.base = (B - 3) * chain.per
            for j in range(CPB + 2):
                turn(B - 1, j)

        def heads(g):
            return [8 * (g // 2) + g % 2 + 2 * n for n in range(HG)]

        def states_through(b, j, back):
            return (CPB - 1) * b + max(j + 1 - back, 0)

        order = [("q", 0)]
        for cc in range(NCH):
            if cc + 1 < NCH:
                order.append(("q", cc + 1))
            if cc >= 2:
                order.append(("xn", cc - 2))
            if (cc + 1) % CPB:
                order.append(("qs", cc + 1))
        order += [("xn", NCH - 2), ("xn", NCH - 1)]
        place = {what: 2 * n for n, what in enumerate(order)}
        turned_per_batch = 2 * (3 * CPB - 1)
        for kind in ("q", "qs", "xn"):
            for cc in range(CPB + 2 if kind == "xn" else 2 * CPB, NCH - CPB + 1):
                if (kind, cc) in place:
                    assert place[kind, cc] - place[kind, cc - CPB] == turned_per_batch

        def turn_count(kind, b, j):
            if isinstance(b, int):
                return place[kind, b * CPB + j]
            return (b - 1) * turned_per_batch + place[kind, CPB + j]

        block = ctx.enter_context(nc.Block())

        @block.sync
        def _(sp):
            def load_x(b, j):
                c = b * CPB + j
                ge(sp, x1_rdy, c - 3)
                sp.dma_start(x[:, j, :], x_rows[c]).then_inc(x_in[j], 16)
                ge(sp, u_ps, NG * (c - 3))
                sp.dma_start(ctx_t[:, j], t["ctx_t"][c]).then_inc(ct_in[j], 16)

            def load_v(b, j):
                c = b * CPB + j
                ge(sp, u_ps, NG * (c - 1))
                ge(sp, ds_ps, 2 * states_through(b, j, 2))
                sp.dma_start(ctx_v[:, j % 2, :, 0:DH], ctx_rows[c]).then_inc(cv_in[j % 2], 16)

            def stage_a(part, b, j):
                c = b * CPB + j
                if part == 1:
                    if isinstance(c, int) and c == 0:
                        load_x(0, 0)
                        load_x(0, 1)
                    load_v(b, j)
                    nb, nj = (b, j + 1) if j + 1 < CPB else (b + 1, 0)
                    if not (isinstance(nb, int) and nb >= B) and not (isinstance(c, int) and c == 0):
                        load_x(nb, nj)
                if part == 4:
                    ge(sp, neg_g_rdy, c + 1)
                    sp.dma_start(t["g_row"], neg_g[:, :]).then_inc(g_out, 16)
                    sp.wait_ge(g_out, 16 * c + 16)
                    ge(sp, d_rdy, NH * c)
                    sp.dma_start(gb[:, :, :], t["g_row"].rearrange("h s -> (h s)").partition_broadcast(P)
                                 ).then_inc(gb_in, 16)

            def stage_e(part, b, j):
                c = b * CPB + j
                if part == 1:
                    ge(sp, x1_rdy, c + 1)
                    sp.dma_start(x1_rows[c], x1[:, j % 2, :]).then_inc(x1_out[j % 2], 16)
                if part == 2:
                    ge(sp, xn_rdy, c + 1)
                    sp.dma_start(xn_rows[c], xn[:, j % 2, :]).then_inc(xn_out[j % 2], 16)

            sp.dma_start(w_gate[:, :, :], t["w_gate"].rearrange("(k p) n -> p k n", p=P)).then_inc(const_in, 16)
            sp.dma_start(gate_bias[:, :], t["gate_bias"].partition_broadcast(P)).then_inc(const_in, 16)
            sp.dma_start(rw[:, :, :], t["rw"].rearrange("(k p) n -> p k n", p=P)).then_inc(const_in, 16)
            sp.dma_start(lns[:, :], t["ln_scale"].partition_broadcast(P)).then_inc(const_in, 16)
            sp.dma_start(gx[:, 0:1], t["g_xattn"].partition_broadcast(P)).then_inc(const_in, 16)
            sp.dma_start(gx[:, 1:2], t["g_ffn"].partition_broadcast(P)).then_inc(const_in, 16)
            weights_in(sp, keep, expert_weights(t, NE, 0), slice(0, 3), stage_in)
            sp.wait_ge(pool_set, 1)
            sp.dma_start(t["lists"].rearrange("(p n) o -> p (n o)", p=P), zero_i[:, :]).then_inc(table_in, 16)
            schedule(sp, None, {"A": stage_a, "E": stage_e}, sp.Fori)
            for done in stage_in:
                sp.wait_ge(done, 16)
            for n in range(2):
                sp.wait_ge(x1_out[n], 16 * NCH // 2)
                sp.wait_ge(xn_out[n], 16 * NCH // 2)

        @block.gpsimd
        def _(pool):
            nc.gpsimd.memset(zero_i[:, :], 0).then_inc(pool_set, 1)
            nc.gpsimd.memset(ident[:, :], 0.0).then_inc(pool_set, 1)
            nc.gpsimd.memset(upper[:, :], 1.0).then_inc(pool_set, 1)
            nc.gpsimd.memset(headmask[:, :], 1.0).then_inc(pool_set, 1)
            nc.gpsimd.memset(mhalf[:, :], -0.5).then_inc(pool_set, 1)
            pool.wait_ge(pool_set, 5)
            nc.gpsimd.affine_select(out=ident[:, :], in_=ident[:, :], compare_op=ALU.not_equal, fill=1.0,
                                    base=0, pattern=[[-1, P]], channel_multiplier=1).then_inc(pool_set, 1)
            nc.gpsimd.affine_select(out=upper[:, :], in_=upper[:, :], compare_op=ALU.is_gt, fill=0.0,
                                    base=0, pattern=[[1, P]], channel_multiplier=-1).then_inc(pool_set, 1)
            nc.gpsimd.affine_select(out=headmask[:, :], in_=headmask[:, :], compare_op=ALU.is_ge, fill=0.0,
                                    base=0, pattern=[[-2, KD]], channel_multiplier=1).then_inc(pool_set, 1)
            pool.wait_ge(pool_set, 8)
            nc.gpsimd.affine_select(out=headmask[:, :], in_=headmask[:, :], compare_op=ALU.is_ge, fill=0.0,
                                    base=1, pattern=[[2, KD]], channel_multiplier=-1).then_inc(pool_set, 1)
            nc.gpsimd.iota(tok_all[:, :], pattern=[[P, NCH]], base=0, channel_multiplier=1).then_inc(pool_set, 1)
            nc.gpsimd.iota(iota_e[:, :], pattern=[[1, NE]], base=0, channel_multiplier=0,
                           allow_small_or_imprecise_dtypes=True).then_inc(pool_set, 1)
            pool.wait_ge(table_in, 16)

            def stage_l(part, b, j):
                c = b * CPB + j
                ge(pool, var1, c + 1)
                nc.gpsimd.tensor_tensor(rs1[:, 1:2], rs1[:, 0:1], mhalf[:, 0:1], ALU.pow).then_inc(rs1_rdy, 1)

            def stage_a(part, b, j):
                c = b * CPB + j
                if part == 7:
                    ge_apart(pool, past, (gb_in, 16 * c + 16))
                    nc.gpsimd.affine_select(out=gb[:, :, :], in_=gb[:, :, :], compare_op=ALU.is_ge, fill=-1.0e30,
                                            base=0, pattern=[[0, NH], [1, P]], channel_multiplier=-1
                                            ).then_inc(gb_rdy, 1)
                if part == 8 and j < CPB - 1:
                    ge(pool, cols_rdy, 2 * c + 2)
                    pool.wait_ge(cv_in[j % 2], 16 * (2 * b + j // 2) + 16)
                    ge(pool, ds_ps, 2 * ((CPB - 1) * b + j))
                    nc.gpsimd.tensor_tensor(ks[:, :, :], ctx_v[:, j % 2, :, 0:DH],
                                            cols[:, j, 1, :, None].to_broadcast([P, NH, DH]),
                                            ALU.mult).then_inc(ks_rdy, 1)

            def stage_c(part, b, j):
                c = b * CPB + j
                if part == 2:
                    ge(pool, var_rdy, c + 1)
                    nc.gpsimd.tensor_tensor(var[:, 2, :], var[:, 1, :], mhalf[:, :], ALU.pow).then_inc(hrs_rdy, 1)

            def stage_d(part, b, j):
                c = b * CPB + j
                if part == 1:
                    ge(pool, o_rdy, c + 1)
                    o = sq[:, :, :].rearrange("p h d -> p (h d)")
                    nc.gpsimd.tensor_tensor(o, o, lns[:, :], ALU.mult).then_inc(scaled_rdy, 1)

            def stage_e(part, b, j):
                c = b * CPB + j
                if part == 1:
                    ge(pool, var2, c + 1)
                    nc.gpsimd.tensor_tensor(rs2[:, 1:2], rs2[:, 0:1], mhalf[:, 0:1], ALU.pow).then_inc(rs2_rdy, 1)
                if part == 4:
                    ge(pool, pos_rdy, c + 1)
                    for k, done in ((0, scat0), (1, scat1)):
                        ge_apart(pool, past, (done, 16 * c))
                        nc.gpsimd.indirect_dma_start(
                            out=t["lists"], out_offset=bass.IndirectOffsetOnAxis(ap=posi[:, j % 2, k:k + 1], axis=0),
                            in_=tok[:, j % 2:j % 2 + 1], in_offset=None).then_inc(done, 16)

            schedule(pool, None, {"L": stage_l, "A": stage_a, "C": stage_c, "D": stage_d, "E": stage_e}, pool.Fori)
            pool.wait_ge(scat0, 16 * NCH)
            pool.wait_ge(scat1, 16 * NCH)

        @block.scalar
        def _(act):
            act.wait_ge(const_in, 96)
            nc.scalar.activation(gx[:, :], gx[:, :], ACT.Tanh).then_inc(act_set, 1)
            act.wait_ge(act_set, 1)
            nc.scalar.activation(lns[:, :], lns[:, :], ACT.Copy, scale=gx[:, 0:1]).then_inc(act_set, 1)
            nc.scalar.activation(keep["tgf"][:, :], gx[:, 1:2], ACT.Copy).then_inc(act_set, 1)

            def turned(before, n, dst):
                act.wait_ge(tr_ps, before + n + 1)
                nc.scalar.activation(dst, p_tr[n][:, :, :], ACT.Copy).then_inc(tr_sb, 1)

            def stage_a(part, b, j):
                c = b * CPB + j
                if part == 2:
                    for n in range(2):
                        if n == 0:
                            ge(act, u_ps, NG * (c - 1))
                        turned(turn_count("q", b, j), n, q_t[:, j % 2, 4 * n:4 * n + 4, :])
                if part == 3:
                    ge(act, absf_rdy, c + 1)
                    nc.scalar.activation(lnf[:, 0, :], absf[:, :], ACT.Exp, scale=-1.0).then_inc(lnf_rdy, 1)
                    act.wait_ge(lnf_rdy, 2 * c + 1)
                    nc.scalar.activation(lnf[:, 1, :], lnf[:, 0, :], ACT.Ln, bias=1.0).then_inc(lnf_rdy, 1)
                if part == 5:
                    ge(act, cols_ps, c + 1)
                    nc.scalar.activation(cols[:, j, 0, :], p_row[:, 256:256 + NH], ACT.Copy).then_inc(cols_rdy, 1)
                    lo, hi = (1, 3) if j == 0 else (2, 4) if j == CPB - 1 else (1, 4)
                    nc.scalar.activation(cols[:, j, lo:hi, :].rearrange("p a h -> p (a h)"),
                                         p_row[:, 256 + lo * NH:256 + hi * NH], ACT.Exp).then_inc(cols_rdy, 1)
                    if 0 < j < CPB - 1:
                        act.wait_ge(rows_rdy, c + 1)
                        nc.scalar.activation(dec[:, 1:2], dec[:, 0:1], ACT.Exp).then_inc(dec_rdy, 1)
                if part == 7:
                    ge(act, gb_rdy, c + 1)
                    act.wait_ge(cols_rdy, 2 * c + 2)
                    ge(act, c_rdy, NG * (c - 1))
                    for h in heads(0) + heads(1) + heads(2) + heads(3):
                        nc.scalar.activation(dmat[:, j % 2, h, :], gb[:, h, :], ACT.Exp,
                                             bias=cols[:, j, 0, h:h + 1]).then_inc(d_rdy, 1)
                if part == 8 and j > 0:
                    for n in range(2):
                        if n == 0:
                            ge(act, u_ps, NG * c)
                        turned(turn_count("qs", b, j), n, qs_t[:, 4 * n:4 * n + 4, :])

            def stage_b(part, b, j):
                c = b * CPB + j
                if part > 0:
                    g = part - 1
                    act.wait_ge(u_ps, NG * c + g + 1)
                    ge(act, o_rdy, c - 1)
                    nc.scalar.activation(uc[:, j % 2, heads(g)[0]:heads(g)[-1] + 1:2, :],
                                         p_u[g % 2][:, 0:HG * HV].rearrange("p (h d) -> p h d", d=HV),
                                         ACT.Copy).then_inc(u_rdy, 1)

            def stage_c(part, b, j):
                c = b * CPB + j
                if part == 1:
                    act.wait_ge(cen_rdy, c + 1)
                    nc.scalar.activation(sq[:, :, :], uc[:, j % 2, :, 0:DH], ACT.Square).then_inc(sq_rdy, 1)

            def stage_e(part, b, j):
                c = b * CPB + j
                if part == 2:
                    ge(act, lg_ps, c)
                    for n in range(2):
                        turned(turn_count("xn", b, j), n, xn_t[:, 4 * n:4 * n + 4, :])
                if part == 3:
                    ge(act, top_rdy, c + 1)
                    nc.scalar.activation(ew[:, 1:2], ew[:, 0:1], ACT.Exp).then_inc(ew_rdy, 1)

            schedule(act, None, {"A": stage_a, "B": stage_b, "C": stage_c, "E": stage_e}, act.Fori)

        @block.vector
        def _(dve):
            chain = Chain(dve, dve_steps)
            chain.per = DVE_PER_BATCH
            step, settle, link = chain.step, chain.settle, chain.link

            nc.vector.memset(ones[:, :], 1.0).then_inc(dve_set, 1)
            nc.vector.memset(one_row[:, :], 1.0).then_inc(dve_set, 1)
            nc.vector.memset(zero_row[:, :], 0.0).then_inc(dve_set, 1)
            nc.vector.memset(hot_acc[:, :], 0.0).then_inc(dve_set, 1)
            for n in range(2):
                nc.vector.memset(ctx_v[:, n, :, DH:HV], 1.0).then_inc(dve_set, 1)
            dve.wait_ge(pool_set, 11)
            idv = ident[0:NH, 0:NH].rearrange("p (j o) -> p o j", o=2)
            nc.vector.tensor_reduce(out=headsel[:, 0:1], in_=idv[:, 0, :], axis=AX.X, op=ALU.add).then_inc(dve_set, 1)
            nc.vector.tensor_reduce(out=headsel[:, DH:DH + 1], in_=idv[:, 1, :], axis=AX.X, op=ALU.add).then_inc(dve_set, 1)
            dve.wait_ge(dve_set, 8)
            for o in (0, DH):
                nc.vector.tensor_copy(headsel[:, o + 1:o + DH], headsel[:, o:o + 1].to_broadcast([NH, DH - 1])
                                      ).then_inc(dve_set, 1)
            dve.wait_ge(const_in, 96)
            nc.vector.tensor_tensor(w_gate[:, KD:2 * KD, :], w_gate[:, KD:2 * KD, :], w_gate[:, 2 * KD:3 * KD, :],
                                    ALU.add).then_inc(dve_set, 1)
            dve.wait_ge(dve_set, 11)

            def stage_l(part, b, j):
                c = b * CPB + j
                if True:
                    dve.wait_ge(x_in[j], 16 * b + 16)
                    step(nc.vector.bn_stats(st1[:, 0, :], x[:, j, 0:512]))
                    step(nc.vector.bn_stats(st1[:, 1, :], x[:, j, 512:1024]))
                    chain.settle_apart(past)
                    link(nc.vector.bn_aggr(mv1[:, :], st1[:, :, :].rearrange("p a b -> p (a b)")))
                    nc.vector.tensor_scalar(rs1[:, 0:1], mv1[:, 1:2], LN_EPS, None, ALU.add).then_inc(var1, 1)

            def stage_a(part, b, j):
                c = b * CPB + j
                if part == 2:
                    dve.wait_ge(rs1_rdy, c + 1)
                    ge(dve, gates_ps, c)
                    ge(dve, qs_rdy, (CPB - 1) * b + max(j - 1, 0))
                    nc.vector.tensor_scalar(q[:, :, :].rearrange("p h d -> p (h d)"), x[:, j, :], mv1[:, 0:1], rs1[:, 1:2],
                                            ALU.subtract, ALU.mult).then_inc(q_rdy, 1)
                if part == 3:
                    dve.wait_ge(gates_ps, c + 1)
                    link(nc.vector.tensor_tensor(gates[:, :], p_gate[:, 0:2 * NH], gate_bias[:, :], ALU.add))
                    f = gates[:, NH:2 * NH]
                    nc.vector.scalar_tensor_tensor(out=absf[:, :], in0=f, scalar=-1.0, in1=f, op0=ALU.mult,
                                                   op1=ALU.max).then_inc(absf_rdy, 1)
                if part == 4:
                    f = gates[:, NH:2 * NH]
                    dve.wait_ge(lnf_rdy, 2 * c + 2)
                    dve.wait_ge(absf_rdy, c + 1)
                    nc.vector.scalar_tensor_tensor(out=f, in0=f, scalar=0.0, in1=lnf[:, 1, :], op0=ALU.min,
                                                   op1=ALU.subtract).then_inc(lf_rdy, 1)
                    dve.wait_ge(gt_ps, c + 1)
                    ge(dve, cols_ps, c)
                    now, was = j % 2, (j + 1) % 2
                    f0 = 0.0 if j == 0 else fcum[:, was, P - 1:P]
                    g0 = NEG if j == 0 else gmax[:, was, P - 1:P]
                    link(nc.vector.tensor_tensor_scan(fcum[:, now, :], one_row[:, :], p_row[0:NH, P:2 * P], f0,
                                                      ALU.mult, ALU.add))
                    link(nc.vector.tensor_tensor(rows[:, 0, :], p_row[0:NH, 0:P], fcum[:, now, :], ALU.subtract))
                    link(nc.vector.tensor_tensor_scan(gmax[:, now, :], zero_row[:, :], rows[:, 0, :], g0,
                                                      ALU.add, ALU.max))
                    ge(dve, g_out, 16 * c)
                    nc.vector.tensor_scalar(neg_g[:, :], gmax[:, now, :], -1.0, None, ALU.mult).then_inc(neg_g_rdy, 1)
                    step(nc.vector.tensor_scalar(rows[:, 1, :], rows[:, 0, :], gmax[:, now, P - 1:P], None, ALU.subtract))
                    if 0 < j < CPB - 1:
                        step(nc.vector.tensor_tensor(dec[:, 0:1], gmax[:, was, P - 1:P], gmax[:, now, P - 1:P], ALU.subtract))
                    if j > 0:
                        dve.wait_ge(neg_g_rdy, c + 1)
                        step(nc.vector.tensor_scalar(rows[:, 3, :], neg_g[:, :], gmax[:, was, P - 1:P], None, ALU.add))
                    nc.vector.scalar_tensor_tensor(out=rows[:, 2, :], in0=fcum[:, now, :], scalar=-1.0,
                                                   in1=gmax[:, now, :], op0=ALU.mult, op1=ALU.subtract
                                                   ).then_inc(rows_rdy, 1)
                if part == 6 and 0 < j < CPB - 1:
                    if True:
                        n = (CPB - 2) * b + j
                        dve.wait_ge(dec_rdy, n)
                        ge(dve, dec_ps, n - 1)
                        nc.vector.tensor_scalar(decm[:, :], headmask[:, :], dec[:, 1:2], None, ALU.mult).then_inc(decm_rdy, 1)
                if part == 8 and j > 0:
                    dve.wait_ge(cols_rdy, 2 * c + 2)
                    link(nc.vector.tensor_scalar(qfac[:, :], cols[:, j, 3, :], DH ** -0.5, None, ALU.mult))
                    nc.vector.tensor_tensor(qs[:, :, :], q[:, :, :], qfac[:, :, None].to_broadcast([P, NH, DH]),
                                            ALU.mult).then_inc(qs_rdy, 1)

            def stage_b(part, b, j):
                c = b * CPB + j
                if part < NG:
                    g = part
                    dve.wait_ge(d_rdy, NH * c + HG * (g + 1))
                    dve.wait_ge(sc_ps, NG * c + g + 1)
                    ge(dve, u_ps, NG * c + g - 1)
                    nc.vector.scalar_tensor_tensor(
                        out=cmat[:, g % 2, :, :], in0=p_sc[:, :, :],
                        scalar=DH ** -0.5, in1=dmat[:, j % 2, heads(g)[0]:heads(g)[-1] + 1:2, :],
                        op0=ALU.mult, op1=ALU.mult).then_inc(c_rdy, 1)
                if part == 4 and j < CPB - 1:
                    n = (CPB - 1) * b + j
                    if j > 0:
                        dve.wait_ge(dec_ps, (CPB - 2) * b + j)
                        dve.wait_ge(u_ps, NG * c + NG)
                        link(nc.vector.tensor_tensor(state[:, :, :], state[:, :, :],
                                                     p_gate[:, 64 + 64 * (j % 2):64 + 64 * (j % 2) + KD, None].to_broadcast([P, KD, HV]), ALU.mult))
                    for m in range(2):
                        half = state[:, 4 * m:4 * m + 4, :].rearrange("p j d -> p (j d)")
                        dve.wait_ge(ds_ps, 2 * n + m + 1)
                        if j > 0:
                            ins = nc.vector.tensor_tensor(half, half, p_u[m][:, 0:4 * HV], ALU.add)
                        else:
                            ins = nc.vector.tensor_copy(half, p_u[m][:, 0:4 * HV])
                        ins.then_inc(state_rdy, 1)

            def stage_c(part, b, j):
                c = b * CPB + j
                u = uc[:, j % 2, :, 0:DH]
                if part == 1:
                    dve.wait_ge(u_rdy, NG * c + NG)
                    den = uc[:, j % 2, :, DH]
                    link(nc.vector.scalar_tensor_tensor(out=nrm[:, 0, :], in0=den, scalar=-1.0, in1=den,
                                                        op0=ALU.mult, op1=ALU.max))
                    link(nc.vector.tensor_tensor(nrm[:, 0, :], nrm[:, 0, :], cols[:, j, 2, :], ALU.max))
                    link(nc.vector.tensor_scalar(nrm[:, 0, :], nrm[:, 0, :], H_EPS, None, ALU.add))
                    link(nc.vector.reciprocal(nrm[:, 1, :], nrm[:, 0, :]))
                    link(nc.vector.tensor_tensor(u, u, nrm[:, 1, :, None].to_broadcast([P, NH, DH]), ALU.mult))
                    link(nc.vector.tensor_reduce(out=mu[:, 0, :], in_=u, axis=AX.X, op=ALU.add))
                    link(nc.vector.tensor_scalar(mu[:, 1, :], mu[:, 0, :], 1.0 / DH, None, ALU.mult))
                    ge(dve, x1_rdy, c)
                    nc.vector.tensor_tensor(u, u, mu[:, 1, :, None].to_broadcast([P, NH, DH]), ALU.subtract
                                            ).then_inc(cen_rdy, 1)
                if part == 2:
                    dve.wait_ge(sq_rdy, c + 1)
                    link(nc.vector.tensor_reduce(out=var[:, 0, :], in_=sq[:, :, :], axis=AX.X, op=ALU.add))
                    nc.vector.tensor_scalar(var[:, 1, :], var[:, 0, :], 1.0 / DH, H_EPS, ALU.mult, ALU.add
                                            ).then_inc(var_rdy, 1)

            def stage_d(part, b, j):
                c = b * CPB + j
                u = uc[:, j % 2, :, 0:DH]
                if part == 1:
                    dve.wait_ge(hrs_rdy, c + 1)
                    nc.vector.tensor_tensor(sq[:, :, :], u, var[:, 2, :, None].to_broadcast([P, NH, DH]), ALU.mult
                                            ).then_inc(o_rdy, 1)

            def stage_e(part, b, j):
                c = b * CPB + j
                if part == 1:
                    dve.wait_ge(scaled_rdy, c + 1)
                    ge(dve, x1_out[j % 2], 16 * (2 * b + j // 2))
                    nc.vector.tensor_tensor(x1[:, j % 2, :], x[:, j, :], sq[:, :, :].rearrange("p h d -> p (h d)"),
                                            ALU.add).then_inc(x1_rdy, 1)
                    dve.wait_ge(x1_rdy, c + 1)
                    step(nc.vector.bn_stats(st2[:, 0, :], x1[:, j % 2, 0:512]))
                    step(nc.vector.bn_stats(st2[:, 1, :], x1[:, j % 2, 512:1024]))
                    chain.settle_apart(past)
                    link(nc.vector.bn_aggr(mv2[:, :], st2[:, :, :].rearrange("p a b -> p (a b)")))
                    nc.vector.tensor_scalar(rs2[:, 0:1], mv2[:, 1:2], LN_EPS, None, ALU.add).then_inc(var2, 1)
                if part == 2:
                    dve.wait_ge(rs2_rdy, c + 1)
                    ge(dve, xn_out[j % 2], 16 * (2 * b + j // 2))
                    nc.vector.tensor_scalar(xn[:, j % 2, :], x1[:, j % 2, :], mv2[:, 0:1], rs2[:, 1:2],
                                            ALU.subtract, ALU.mult).then_inc(xn_rdy, 1)
                if part == 3:
                    dve.wait_ge(lg_ps, c + 1)
                    step(nc.vector.tensor_copy(lg[:, :], p_rt[:, 0:NE]))
                    chain.settle_apart(past)
                    step(nc.vector.max(mx[:, :], lg[:, :]))
                    chain.settle_apart(past)
                    link(nc.vector.max_index(ix[:, :], mx[:, :], lg[:, :]))
                    nc.vector.tensor_tensor(ew[:, 0:1], mx[:, 1:2], mx[:, 0:1], ALU.subtract).then_inc(top_rdy, 1)
                    ecol = eidx[:, bass.ds(2 * c, 2)]
                    step(nc.vector.tensor_copy(ecol, ix[:, 0:2]))
                    link(nc.vector.tensor_copy(posf[:, :], ix[:, 0:2]))
                    for k in range(2):
                        step(nc.vector.tensor_scalar(hot[:, k, :], iota_e[:, :], posf[:, k:k + 1], None, ALU.is_equal))
                    settle()
                    nc.vector.tensor_tensor(hot[:, 2, :], hot[:, 0, :], hot[:, 1, :], ALU.add).then_inc(hot_rdy, 1)
                if part == 4:
                    dve.wait_ge(rank_ps, c + 1)
                    for k in range(2):
                        step(nc.vector.scalar_tensor_tensor(out=scr[:, k, :], in0=p_rt[:, 32:32 + NE], scalar=1.0,
                                                            in1=hot[:, k, :], op0=ALU.mult, op1=ALU.mult))
                    step(nc.vector.tensor_tensor(hot_acc[:, :], hot_acc[:, :], hot[:, 2, :], ALU.add))
                    settle()
                    link(nc.vector.tensor_reduce(out=rank[:, bass.ds(2 * c, 2)], in_=scr[:, :, :], axis=AX.X, op=ALU.add))
                    ge(dve, scat0, 16 * (c - 1))
                    ge(dve, scat1, 16 * (c - 1))
                    step(nc.vector.tensor_copy(tok[:, j % 2:j % 2 + 1], tok_all[:, bass.ds(c, 1)]))
                    nc.vector.scalar_tensor_tensor(out=posi[:, j % 2, :], in0=posf[:, :], scalar=float(CAP),
                                                   in1=rank[:, bass.ds(2 * c, 2)], op0=ALU.mult, op1=ALU.add
                                                   ).then_inc(pos_rdy, 1)
                    dve.wait_ge(ew_rdy, c + 1)
                    link(nc.vector.tensor_scalar(ew[:, 2:3], ew[:, 1:2], 1.0, None, ALU.add))
                    link(nc.vector.reciprocal(wts[:, bass.ds(2 * c, 1)], ew[:, 2:3]))
                    step(nc.vector.tensor_scalar(wts[:, bass.ds(2 * c + 1, 1)], ew[:, 1:2], wts[:, bass.ds(2 * c, 1)], None, ALU.mult))

            schedule(dve, chain, {"L": stage_l, "A": stage_a, "B": stage_b, "C": stage_c, "D": stage_d, "E": stage_e}, dve.Fori)
            settle()
            dve.wait_ge(rank_ps, NCH)
            dve.wait_ge(hot_rdy, NCH)

        @block.tensor
        def _(pe):
            pe.wait_ge(pool_set, 11)
            pe.wait_ge(dve_set, 11)
            pe.wait_ge(const_in, 96)

            def turn_tile(src, dst):
                for k in range(4):
                    last = nc.tensor.transpose(p_tr[dst][:, k, :], src[:, k * P:(k + 1) * P], ident[:, :])
                last.then_inc(tr_ps, 1)

            def p_tr_free(kind, b, j):
                ge(pe, tr_sb, turn_count(kind, b, j))

            def stage_a(part, b, j):
                c = b * CPB + j
                if part == 2:
                    pe.wait_ge(q_rdy, c + 1)
                    p_tr_free("q", b, j)
                    flat = q[:, :, :].rearrange("p h d -> p (h d)")
                    for n in range(2):
                        turn_tile(flat[:, 512 * n:512 * n + 512], n)
                if part == 3:
                    pe.wait_ge(ct_in[j], 16 * b + 16)
                    ge(pe, lf_rdy, c)
                    ge(pe, state_rdy, 2 * states_through(b, j, 2))
                    pe.wait_ge(tr_sb, turn_count("q", b, j) + 2)
                    for k in range(2 * KD):
                        lhs = q_t[:, j % 2, k, :] if k < KD else ctx_t[:, j, k - KD, :]
                        last = nc.tensor.matmul(p_gate[:, 0:2 * NH], lhs, w_gate[:, k, :], start=(k == 0),
                                                stop=(k == 2 * KD - 1))
                    last.then_inc(gates_ps, 1)
                if part == 4:
                    pe.wait_ge(lf_rdy, c + 1)
                    ge(pe, cols_rdy, 2 * c)
                    for m in range(2):
                        last = nc.tensor.transpose(p_row[0:NH, m * P:(m + 1) * P], gates[:, m * NH:(m + 1) * NH], ident[:, :])
                    last.then_inc(gt_ps, 1)
                if part == 5:
                    ge_apart(pe, past, (rows_rdy, c + 1))
                    which = [r for r in range(4) if not (r == 1 and j == CPB - 1) and not (r == 3 and j == 0)]
                    for r in which:
                        last = nc.tensor.transpose(p_row[:, 256 + r * NH:256 + (r + 1) * NH], rows[:, r, :], ident[0:NH, 0:NH])
                    last.then_inc(cols_ps, 1)
                if part == 6 and 0 < j < CPB - 1:
                    if True:
                        pe.wait_ge(decm_rdy, (CPB - 2) * b + j)
                        nc.tensor.matmul(p_gate[:, 64 + 64 * (j % 2):64 + 64 * (j % 2) + KD], headsel[:, :], decm[:, :], start=True, stop=True
                                         ).then_inc(dec_ps, 1)
                if part == 8 and j > 0:
                    pe.wait_ge(qs_rdy, (CPB - 1) * b + j)
                    p_tr_free("qs", b, j)
                    flat = qs[:, :, :].rearrange("p h d -> p (h d)")
                    for n in range(2):
                        turn_tile(flat[:, 512 * n:512 * n + 512], n)

            def scores(b, j, g):
                c = b * CPB + j
                ge(pe, c_rdy, NG * c + g)
                for n, h in enumerate(heads(g)):
                    lo = DH * (h % 2)
                    last = nc.tensor.matmul(p_sc[:, n, :], ctx_t[lo:lo + DH, j, h // 2, :],
                                            q_t[lo:lo + DH, j % 2, h // 2, :], start=True, stop=True)
                last.then_inc(sc_ps, 1)

            def values(b, j, g):
                c = b * CPB + j
                pe.wait_ge(c_rdy, NG * c + g + 1)
                ge(pe, u_rdy, NG * c + g - 1)
                if g < 2:
                    ge(pe, state_rdy, 2 * states_done(b, j))
                for n, h in enumerate(heads(g)):
                    lo = DH * (h % 2)
                    out = p_u[g % 2][:, n * HV:(n + 1) * HV]
                    last = nc.tensor.matmul(out, cmat[:, g % 2, n, :], ctx_v[:, j % 2, h, :], start=True, stop=(j == 0))
                    if j > 0:
                        last = nc.tensor.matmul(out, qs_t[lo:lo + DH, h // 2, :], state[lo:lo + DH, h // 2, :],
                                                start=False, stop=True)
                last.then_inc(u_ps, 1)

            def states_done(b, j):
                return (CPB - 1) * b + j

            def stage_b(part, b, j):
                c = b * CPB + j
                if part == 0:
                    scores(b, j, 0)
                if part == 1:
                    scores(b, j, 1)
                    if j > 0:
                        pe.wait_ge(tr_sb, turn_count("qs", b, j) + 2)
                    pe.wait_ge(cv_in[j % 2], 16 * (2 * b + j // 2) + 16)
                    values(b, j, 0)
                if part == 2:
                    scores(b, j, 2)
                    values(b, j, 1)
                if part == 3:
                    scores(b, j, 3)
                    values(b, j, 2)
                if part == 4:
                    values(b, j, 3)
                    if j < CPB - 1:
                        pe.wait_ge(ks_rdy, states_done(b, j) + 1)
                        for m in range(2):
                            pe.wait_ge(u_rdy, NG * c + 3 + m)
                            for n in range(8):
                                h = 8 * m + n
                                lo = DH * (h % 2)
                                last = nc.tensor.matmul(p_u[m][lo:lo + DH, (n // 2) * HV:(n // 2 + 1) * HV],
                                                        ks[:, h, :], ctx_v[:, j % 2, h, :], start=True, stop=True)
                            last.then_inc(ds_ps, 1)

            def stage_e(part, b, j):
                c = b * CPB + j
                if part == 2:
                    pe.wait_ge(xn_rdy, c + 1)
                    p_tr_free("xn", b, j)
                    for n in range(2):
                        turn_tile(xn[:, j % 2, 512 * n:512 * n + 512], n)
                if part == 3:
                    pe.wait_ge(tr_sb, turn_count("xn", b, j) + 2)
                    ge(pe, pos_rdy, c)
                    for k in range(KD):
                        last = nc.tensor.matmul(p_rt[:, 0:NE], xn_t[:, k, :], rw[:, k, :], start=(k == 0),
                                                stop=(k == KD - 1))
                    last.then_inc(lg_ps, 1)
                if part == 4:
                    pe.wait_ge(hot_rdy, c + 1)
                    nc.tensor.matmul(p_rt[:, 32:32 + NE], upper[:, :], hot[:, 2, :], start=True, stop=False)
                    nc.tensor.matmul(p_rt[:, 32:32 + NE], ones[:, :], hot_acc[:, :], start=False, stop=True
                                     ).then_inc(rank_ps, 1)

            schedule(pe, None, {"A": stage_a, "B": stage_b, "E": stage_e}, pe.Fori)



def expert_weights(t, e, shared_half=0):
    if isinstance(e, int) and e == NE:
        part = slice(shared_half * FE, (shared_half + 1) * FE)
        return t["sg"][:, part], t["su"][:, part], t["sd"][part, :]
    return tuple(t[n][bass.ds(e, 1)].rearrange("o a b -> (o a) b") for n in ("eg", "eu", "ed"))


def weights_in(eng, keep, matrices, which, done):
    stage = keep["stage"]
    places = (stage[:, 0:GUP, 0:FE], stage[:, 0:GUP, FE:D], stage[:, GUP:PIECES, :])
    for place, matrix, sem in zip(places[which], matrices[which], done):
        eng.dma_start(place, matrix.rearrange("(k p) f -> p k f", p=P)).then_inc(sem, 16)


def ffn_block(nc, t, keep, routed):
    f32, f32r, i32 = mybir.dt.float32, mybir.dt.float32r, mybir.dt.int32
    ACT, AX = mybir.ActivationFunctionType, mybir.AxisListType
    with ExitStack() as ctx:
        tag = "b" if routed else "a"

        def sb(name, shape, dt=f32):
            return ctx.enter_context(nc.sbuf_tensor(f"{name}_{tag}", shape, dt))

        def sem(name):
            return ctx.enter_context(nc.semaphore(f"{name}_{tag}"))

        ident, tgf = keep["ident"], keep["tgf"]
        stage = keep["stage"]
        w_hi, w_lo = sb("w_hi", [P, PIECES, D], f32r), sb("w_lo", [P, PIECES, D], f32r)
        xg = sb("xg", [P, D])
        xt_hi, xt_lo = sb("xt_hi", [P, KD, P], f32r), sb("xt_lo", [P, KD, P], f32r)
        eg = sb("eg", [P, FE])
        g, h = sb("g", [P, FE]), sb("h", [P, FE])
        ht_hi, ht_lo = sb("ht_hi", [P, FE // P, P], f32r), sb("ht_lo", [P, FE // P, P], f32r)
        y = sb("y", [P, D])
        base_row = sb("base_row", [P, D])
        p_x = [ctx.enter_context(nc.psum_tensor(f"p_x{n}_{tag}", [P, 4, P], f32)) for n in range(2)]
        p_g = ctx.enter_context(nc.psum_tensor(f"p_g_{tag}", [P, FE], f32))
        p_up = ctx.enter_context(nc.psum_tensor(f"p_up_{tag}", [P, FE], f32))
        p_h = ctx.enter_context(nc.psum_tensor(f"p_h_{tag}", [P, FE // P, P], f32))
        p_y = [ctx.enter_context(nc.psum_tensor(f"p_y{n}_{tag}", [P, 512], f32)) for n in range(2)]
        if routed:
            r0, r1 = sb("r0", [P, D]), sb("r1", [P, D])
            idx = sb("idx", [P, 1], i32)
            cnt_i = sb("cnt_i", [P, NE], i32)
            cnt_f = sb("cnt_f", [P, 2, NE])
            one_e = sb("one_e", [P, NE])
            starts = sb("starts", [P, NE + 1])
            starts_i = sb("starts_i", [P, 3, NE + 1], i32)
            hot = sb("hot", [P, 2 * NCH, NE])
            slot_f, slot_i = sb("slot_f", [P, 2 * NCH]), sb("slot_i", [P, 2 * NCH], i32)
            ones = sb("ones", [P, P])

        past = sem("past")
        wg_in, wu_in, wd_in = sem("wg_in"), sem("wu_in"), sem("wd_in")
        xs_in = sem("xs_in")
        x_in, idx_in, base_in, y_out, z_out, r0_in, r1_in = (
            sem("x_in"), sem("idx_in"), sem("base_in"), sem("y_out"), sem("z_out"), sem("r0_in"), sem("r1_in"))
        gu_hi, gu_split, d_hi, d_split, own_hi = (
            sem("gu_hi"), sem("gu_split"), sem("d_hi"), sem("d_split"), sem("own_hi"))
        xt_ps, xt_hi_rdy, xt_rdy = sem("xt_ps"), sem("xt_hi_rdy"), sem("xt_rdy")
        g_rdy = sem("g_rdy")
        gu_ps, exp_rdy, gu_free, silu_step, h_rdy = (
            sem("gu_ps"), sem("exp_rdy"), sem("gu_free"), sem("silu_step"), sem("h_rdy"))
        ht_ps, ht_hi_rdy, ht_rdy = sem("ht_ps"), sem("ht_hi_rdy"), sem("ht_rdy")
        y_ps, y_rdy, join_step, z_rdy = sem("y_ps"), sem("y_rdy"), sem("join_step"), sem("z_rdy")
        if routed:
            fill_in = sem("fill_in")
            slot_now = sb("slot_now", [P, 2], i32)
            tab_step, tab_rdy, slots_rdy, slot_step = sem("tab_step"), sem("tab_rdy"), sem("slots_rdy"), sem("slot_step")
            cnt_go, cnt_ps = sem("cnt_go"), sem("cnt_ps")

        shared_e = NE if routed else 0

        def tiles(eng, body, finish):
            if not routed:
                body(0, None, 0, 0, True, None, False)
                body(1, 0, 0, 1, False, "shared", False)
                with eng.Fori(2, NCH - 1) as i:
                    body(i, i - 1, 0, i, False, "shared", False)
                body(NCH - 1, NCH - 2, 0, NCH - 1, False, "shared", True)
                finish(NCH, NCH - 1, 0, NCH)
                return
            eng.wait_ge(tab_rdy, 1)
            body(0, None, 0, None, True, None, False)
            body(1, 0, 0, None, False, "routed", False)
            with eng.Fori(2, start(eng, 1)) as i:
                body(i, i - 1, 0, None, False, "routed", False)
            with eng.Fori(1, NE) as e:
                begin = start(eng, e)
                body(begin, lambda: start(eng, e, 1), e, None, True, "routed", False)
                with eng.Fori(begin + 1, start(eng, e + 1)) as i:
                    body(i, i - 1, e, None, False, "routed", False)
            n = start(eng, NE)
            body(n, lambda: start(eng, NE, 1), NE, 0, True, "routed", False)
            body(n + 1, n, NE, 1, False, "shared", False)
            with eng.Fori(2, NCH - 1) as c:
                body(n + c, n + (c - 1), NE, c, False, "shared", False)
            body(n + (NCH - 1), n + (NCH - 2), NE, NCH - 1, False, "shared", True)
            finish(n + NCH, n + (NCH - 1), NE, NCH)

        def start(eng, e, less=0):
            return eng.value_load(starts_i[0:1, less, bass.ds(e, 1)], min_val=MIN_TILES - less, max_val=MAX_TILES - less)

        xn_rows = t["xn"].rearrange("(c p) d -> c p d", p=P)
        base_rows = (t["z"] if routed else t["x1"]).rearrange("(c p) d -> c p d", p=P)
        z_rows = (t["out"] if routed else t["z"]).rearrange("(c p) d -> c p d", p=P)

        block = ctx.enter_context(nc.Block())

        @block.sync
        def _(sp):
            def load_weights(e):
                ge(sp, gu_split, GUP * e)
                weights_in(sp, keep, expert_weights(t, e, 1), slice(0, 2), (wg_in, wu_in))
                ge(sp, d_split, (PIECES - GUP) * e)
                weights_in(sp, keep, expert_weights(t, e, 1), slice(2, 3), (wd_in,))

            def store_routed(q):
                sp.wait_ge(y_rdy, 2 * q + 2)
                sp.dma_start(t["y"][bass.ds(q * P, P), :], y[:, :]).then_inc(y_out, 16)

            def load_base(c):
                ge(sp, z_rdy, c)
                sp.dma_start(base_row[:, :], base_rows[c]).then_inc(base_in, 16)

            def store_joined(c):
                sp.wait_ge(z_rdy, c)
                sp.dma_start(z_rows[c - 1], y[:, :]).then_inc(z_out, 16)

            if not routed:
                sp.wait_ge(gu_split, GUP)
                sp.wait_ge(d_split, PIECES - GUP)
                weights_in(sp, keep, expert_weights(t, 0), slice(0, 3), (wg_in, wu_in, wd_in))
            if routed:
                sp.wait_ge(tab_rdy, 1)
                load_weights(1)
                with sp.Fori(start(sp, NE), MAX_TILES) as f:
                    sp.dma_start(t["y"][bass.ds(f * P, P), :], base_rows[0]).then_inc(fill_in, 16)
                store_routed(0)
                with sp.Fori(2, start(sp, 1)) as i:
                    store_routed(i - 1)
                with sp.Fori(1, NE - 1) as e:
                    store_routed(start(sp, e, 1))
                    load_weights(e + 1)
                    with sp.Fori(start(sp, e) + 1, start(sp, e + 1)) as i:
                        store_routed(i - 1)
                store_routed(start(sp, NE - 1, 1))
                load_weights(NE)
                with sp.Fori(start(sp, NE - 1) + 1, start(sp, NE)) as i:
                    store_routed(i - 1)
                store_routed(start(sp, NE, 1))
            before = start(sp, NE) if routed else 0

            def load_x(c):
                sp.wait_ge(xt_ps, before + c)
                sp.dma_start(xg[:, :], xn_rows[c]).then_inc(xs_in, 16)

            load_base(0)
            load_x(2)
            with sp.Fori(1, NCH - 2) as c:
                load_x(c + 2)
                load_base(c)
                store_joined(c)
            for c in (NCH - 2, NCH - 1):
                load_base(c)
                store_joined(c)
            store_joined(NCH)
            sp.wait_ge(z_out, 16 * NCH)
            if not routed:
                for done in (wg_in, wu_in, wd_in):
                    sp.wait_ge(done, 16)

        @block.gpsimd
        def _(pool):
            def rows_of(i, e, c, first):
                if c is None:
                    part = e * (CAP // P)
                    if not first:
                        part = nc.s_assert_within(
                            part + (i - first_tile[0]), 0, NE * CAP // P,
                            skip_runtime_bounds_check_because="an expert has CAP // P tiles at most")
                    ge_apart(pool, past, (x_in, 16 * i))
                    pool.dma_start(idx[:, :], list_parts[bass.ds(part, 1)].rearrange("o p w -> (o p) w")
                                   ).then_inc(idx_in, 16)
                ge_apart(pool, past, (idx_in, 16 * i + 16 if c is None else 0), (xt_ps, i))
                if c is None:
                    nc.gpsimd.indirect_dma_start(
                        out=xg[:, :], out_offset=None, in_=t["xn"],
                        in_offset=bass.IndirectOffsetOnAxis(ap=idx[:, :], axis=0)).then_inc(x_in, 16)
                else:
                    pool.dma_start(xg[:, :], xn_rows[c]).then_inc(x_in, 16)

            first_tile = [0]
            list_parts = t["lists"].rearrange("(n p) w -> n p w", p=P)

            def body(i, q, e, c, first, prev, last):
                if first:
                    first_tile[0] = i
                if c is None or isinstance(c, int) and c < 2:
                    rows_of(i, e, c, first)
                if prev == "shared" and routed:
                    gather(c - 1, c)

            def gather(k, c):
                if isinstance(c, int) and c == 1:
                    own = start(pool, NE)
                    filled = pool.value_load(starts_i[0:1, 2, NE:NE + 1], min_val=1, max_val=MAX_TILES)
                    pool.wait_ge(y_out, 16 * own)
                    pool.wait_ge(fill_in, 16 * filled)
                    pool.wait_ge(slots_rdy, 1)
                ge_apart(pool, past, (z_rdy, k))
                for m in range(2):
                    nc.gpsimd.tensor_copy(slot_now[:, m:m + 1], slot_i[:, bass.ds(2 * k + m, 1)]).then_inc(slot_step, 1)
                ge_apart(pool, past, (slot_step, 2 * c))
                for m, (r, done) in enumerate(((r0, r0_in), (r1, r1_in))):
                    nc.gpsimd.indirect_dma_start(
                        out=r[:, :], out_offset=None, in_=t["y"],
                        in_offset=bass.IndirectOffsetOnAxis(ap=slot_now[:, m:m + 1], axis=0)).then_inc(done, 16)

            def finish(i, q, e, c):
                if routed:
                    gather(c - 1, c)

            tiles(pool, body, finish)

        @block.scalar
        def _(act):
            def split_gu(i, e):
                ge(act, wg_in, 16 * e)
                ge(act, wu_in, 16 * e)
                ge(act, gu_ps, i)
                for p in range(DVE_HI, GUP):
                    nc.scalar.activation(w_hi[:, p, :], stage[:, p, :], ACT.Copy).then_inc(gu_hi, 1)

            def split_d(i, e, prev):
                ge(act, wd_in, 16 * e)
                if prev:
                    act.wait_ge(y_ps, 2 * i)
                for p in range(GUP, PIECES):
                    nc.scalar.activation(w_hi[:, p, :], stage[:, p, :], ACT.Copy).then_inc(d_hi, 1)

            def h_high(i):
                act.wait_ge(ht_ps, i)
                nc.scalar.activation(ht_hi[:, :, :], p_h[:, :, :], ACT.Copy).then_inc(ht_hi_rdy, 1)

            def x_high(i):
                act.wait_ge(xt_ps, i + 1)
                for n in range(2):
                    nc.scalar.activation(xt_hi[:, 4 * n:4 * n + 4, :], p_x[n][:, :, :], ACT.Copy).then_inc(xt_hi_rdy, 1)

            def y_copy(q):
                ge(act, y_out, 16 * q)
                for n in range(2):
                    act.wait_ge(y_ps, 2 * q + (n + 1))
                    nc.scalar.activation(y[:, 512 * n:512 * n + 512], p_y[n][:, :], ACT.Copy).then_inc(y_rdy, 1)

            def body(i, q, e, c, first, prev, last):
                if first:
                    split_gu(i, e)
                if prev:
                    h_high(i)
                act.wait_ge(gu_ps, i + 1)
                nc.scalar.activation(g[:, :], p_g[:, :], ACT.Copy).then_inc(g_rdy, 1)
                nc.scalar.activation(eg[:, :], p_g[:, :], ACT.Exp, scale=-1.0).then_inc(exp_rdy, 1)
                if not last:
                    x_high(i + 1)
                if prev == "routed":
                    y_copy(q() if callable(q) else q)
                if first:
                    split_d(i, e, prev)

            x_high(0)
            tiles(act, body, lambda i, q, e, c: h_high(i))

        @block.vector
        def _(dve):
            def split(p, sem_hi, n_hi, sem_lo):
                dve.wait_ge(sem_hi, n_hi)
                nc.vector.tensor_tensor(w_lo[:, p, :], stage[:, p, :], w_hi[:, p, :].bitcast(f32), ALU.subtract
                                        ).then_inc(sem_lo, 1)

            def split_gu(i, e):
                ge(dve, wg_in, 16 * e)
                ge(dve, wu_in, 16 * e)
                ge(dve, gu_ps, i)
                for p in range(DVE_HI):
                    nc.vector.tensor_copy(w_hi[:, p, :], stage[:, p, :]).then_inc(own_hi, 1)
                    split(p, own_hi, DVE_HI * e + p + 1, gu_split)
                for p in range(DVE_HI, GUP):
                    split(p, gu_hi, (GUP - DVE_HI) * e + (p - DVE_HI + 1), gu_split)

            def split_d(e):
                for p in range(GUP, PIECES):
                    split(p, d_hi, (PIECES - GUP) * e + (p - GUP + 1), d_split)

            def h_low(i):
                dve.wait_ge(ht_hi_rdy, i)
                nc.vector.tensor_tensor(ht_lo[:, :, :], p_h[:, :, :], ht_hi[:, :, :].bitcast(f32), ALU.subtract
                                        ).then_inc(ht_rdy, 1)

            def x_low(i):
                for n in range(2):
                    dve.wait_ge(xt_hi_rdy, 2 * i + (n + 1))
                    nc.vector.tensor_tensor(xt_lo[:, 4 * n:4 * n + 4, :], p_x[n][:, :, :],
                                            xt_hi[:, 4 * n:4 * n + 4, :].bitcast(f32), ALU.subtract).then_inc(xt_rdy, 1)

            def product(i):
                dve.wait_ge(g_rdy, i + 1)
                nc.vector.tensor_tensor(h[:, :], g[:, :], p_up[:, :], ALU.mult).then_inc(gu_free, 1)

            def silu(i):
                dve.wait_ge(exp_rdy, i + 1)
                nc.vector.tensor_scalar(eg[:, :], eg[:, :], 1.0, None, ALU.add).then_inc(silu_step, 1)
                dve.wait_ge(silu_step, 2 * i + 1)
                nc.vector.reciprocal(eg[:, :], eg[:, :]).then_inc(silu_step, 1)
                dve.wait_ge(silu_step, 2 * i + 2)
                nc.vector.tensor_tensor(h[:, :], h[:, :], eg[:, :], ALU.mult).then_inc(h_rdy, 1)

            def join(q, c):
                k = c - 1
                dve.wait_ge(base_in, 16 * c)
                if routed:
                    dve.wait_ge(r0_in, 16 * c)
                    nc.vector.tensor_scalar(r0[:, :], r0[:, :], keep["wts"][:, bass.ds(2 * k, 1)], None, ALU.mult
                                            ).then_inc(join_step, 1)
                    dve.wait_ge(r1_in, 16 * c)
                    dve.wait_ge(join_step, 4 * k + 1)
                    nc.vector.scalar_tensor_tensor(out=r0[:, :], in0=r1[:, :], scalar=keep["wts"][:, bass.ds(2 * k + 1, 1)],
                                                   in1=r0[:, :], op0=ALU.mult, op1=ALU.add).then_inc(join_step, 1)
                    dve.wait_ge(join_step, 4 * k + 2)
                    if isinstance(c, int) and c == 1:
                        dve.wait_ge(y_out, 16 * q)
                ge(dve, z_out, 16 * k)
                for n in range(2):
                    half = slice(512 * n, 512 * n + 512)
                    dve.wait_ge(y_ps, 2 * q + (n + 1))
                    src = p_y[n][:, :]
                    if routed:
                        nc.vector.tensor_tensor(r0[:, half], p_y[n][:, :], r0[:, half], ALU.add).then_inc(join_step, 1)
                        dve.wait_ge(join_step, 4 * k + n + 3)
                        src = r0[:, half]
                    last = nc.vector.scalar_tensor_tensor(out=y[:, half], in0=src, scalar=tgf[:, 0:1],
                                                          in1=base_row[:, half], op0=ALU.mult, op1=ALU.add)
                last.then_inc(z_rdy, 1)

            def tables():
                steps = [0]

                def link(ins):
                    ins.then_inc(tab_step, 1)
                    steps[0] += 1
                    dve.wait_ge(tab_step, steps[0])

                link(nc.vector.memset(ones[:, :], 1.0))
                link(nc.vector.memset(one_e[:, :], 1.0))
                link(nc.vector.memset(starts[:, 0:1], 0.0))
                nc.vector.memset(xg[:, 0:1], 0.0).then_inc(cnt_go, 1)
                dve.wait_ge(cnt_ps, 1)
                link(nc.vector.tensor_scalar(cnt_i[:, :], p_y[0][:, 0:NE], float(P - 1), None, ALU.add))
                link(nc.vector.tensor_scalar(cnt_i[:, :], cnt_i[:, :], 7, None, ALU.arith_shift_right))
                link(nc.vector.tensor_scalar(cnt_f[:, 0, :], cnt_i[:, :], float(MIN_TILES), None, ALU.max))
                link(nc.vector.tensor_scalar(cnt_f[:, 0, 0:1], cnt_f[:, 0, 0:1], float(MIN_TILES + 1), None, ALU.max))
                link(nc.vector.tensor_tensor_scan(starts[:, 1:NE + 1], one_e[:, :], cnt_f[:, 0, :], 0.0, ALU.mult, ALU.add))
                link(nc.vector.tensor_copy(starts_i[:, 0, :], starts[:, :]))
                link(nc.vector.tensor_scalar(starts_i[:, 1, :], starts[:, :], -1.0, None, ALU.add))
                link(nc.vector.tensor_scalar(starts_i[:, 2, :], starts[:, :], -1.0, float(MAX_TILES), ALU.mult, ALU.add))
                nc.vector.memset(xg[:, 0:1], 0.0).then_inc(tab_rdy, 1)
                link(nc.vector.tensor_scalar(cnt_f[:, 1, :], starts[:, 0:NE], float(P), None, ALU.mult))
                link(nc.vector.tensor_tensor(hot[:, :, :], keep["iota_e"][:, None, :].to_broadcast([P, 2 * NCH, NE]),
                                             keep["eidx"][:, :, None].to_broadcast([P, 2 * NCH, NE]), ALU.is_equal))
                link(nc.vector.tensor_tensor(hot[:, :, :], hot[:, :, :],
                                             cnt_f[:, 1, None, :].to_broadcast([P, 2 * NCH, NE]), ALU.mult))
                link(nc.vector.tensor_reduce(out=slot_f[:, :], in_=hot[:, :, :], axis=AX.X, op=ALU.add))
                nc.vector.tensor_tensor(slot_i[:, :], slot_f[:, :], keep["rank"][:, :], ALU.add).then_inc(slots_rdy, 1)

            def body(i, q, e, c, first, prev, last):
                if first:
                    split_gu(i, e)
                if prev:
                    h_low(i)
                product(i)
                if not last:
                    x_low(i + 1)
                silu(i)
                if prev == "shared":
                    join(q, c)
                if first:
                    split_d(e)

            def finish(i, q, e, c):
                h_low(i)
                join(q, c)

            if routed:
                tables()
            x_low(0)
            tiles(dve, body, finish)

        @block.tensor
        def _(pe):
            trio = ((xt_hi, w_hi), (xt_lo, w_hi), (xt_hi, w_lo))

            def turn_x(i, c):
                if c is None or isinstance(c, int) and c == 0:
                    pe.wait_ge(x_in, 16 * i + 16)
                else:
                    pe.wait_ge(xs_in, 16 * c)
                for k in range(KD):
                    last = nc.tensor.transpose(p_x[k // 4][:, k % 4, :], xg[:, k * P:(k + 1) * P], ident[:, :])
                last.then_inc(xt_ps, 1)

            def turn_h(i):
                pe.wait_ge(h_rdy, i)
                for k in range(FE // P):
                    last = nc.tensor.transpose(p_h[:, k, :], h[:, k * P:(k + 1) * P], ident[:, :])
                last.then_inc(ht_ps, 1)

            def down(i, e):
                pe.wait_ge(ht_rdy, i)
                for n in range(2):
                    for k in range(FE // P):
                        if n == 0:
                            pe.wait_ge(d_split, (PIECES - GUP) * e + (k + 1))
                        w = slice(512 * n, 512 * n + 512)
                        for m, (a, b) in enumerate(((ht_hi, w_hi), (ht_lo, w_hi), (ht_hi, w_lo))):
                            last = nc.tensor.matmul(p_y[n][:, :], a[:, k, :], b[:, GUP + k, w],
                                                    start=(k == 0 and m == 0), stop=(k == FE // P - 1 and m == 2))
                    last.then_inc(y_ps, 1)

            def body(i, q, e, c, first, prev, last):
                ge(pe, gu_free, i)
                ge(pe, exp_rdy, i)
                for k in range(KD):
                    if k % 4 == 0:
                        pe.wait_ge(xt_rdy, 2 * i + (k // 4 + 1))
                    pe.wait_ge(gu_split, GUP * e + (k + 1))
                    for m, (a, w) in enumerate(trio):
                        for out, o in ((p_g, 0), (p_up, FE)):
                            mm = nc.tensor.matmul(out[:, :], a[:, k, :], w[:, k, o:o + FE],
                                                  start=(k == 0 and m == 0), stop=(k == KD - 1 and m == 2))
                    if k == 3 and prev:
                        turn_h(i)
                mm.then_inc(gu_ps, 1)
                if not last:
                    turn_x(i + 1, c)
                if prev:
                    down(i, e - 1 if first else e)

            def finish(i, q, e, c):
                turn_h(i)
                down(i, e)

            if routed:
                pe.wait_ge(cnt_go, 1)
                nc.tensor.matmul(p_y[0][:, 0:NE], ones[:, :], keep["hot_acc"][:, :], start=True, stop=True).then_inc(cnt_ps, 1)
            turn_x(0, None)
            tiles(pe, body, finish)


def build(nc, t):
    f32 = mybir.dt.float32
    with ExitStack() as ctx:
        shapes = {"stage": [P, PIECES, D], "ident": [P, P], "iota_e": [P, NE], "hot_acc": [P, NE], "tgf": [P, 1],
                  "eidx": [P, 2 * NCH], "rank": [P, 2 * NCH], "wts": [P, 2 * NCH]}
        keep = {n: ctx.enter_context(nc.sbuf_tensor(n, s, f32)) for n, s in shapes.items()}
        mix_block(nc, t, keep)
        ffn_block(nc, t, keep, False)
        ffn_block(nc, t, keep, True)


def kernel(**inputs):
    import numpy as _np
    import concourse.bacc as _bacc
    from concourse import mybir as _mybir
    from concourse.bass_utils import run_bass_kernel_spmd as _run

    a = {k: _np.asarray(v) for k, v in inputs.items()}
    ctx = a["ctx_2048"].reshape(T, D)
    given = {
        "x": a["x"].reshape(T, D),
        "ctx": ctx,
        "ctx_t": ctx.reshape(NCH, P, KD, P).transpose(0, 3, 2, 1),
        "w_gate": _np.concatenate([a["L0_xattn_Wi"], a["L0_xattn_Wf"]], axis=1),
        "gate_bias": _np.concatenate([a["L0_xattn_bi"], a["L0_xattn_bf"]]),
        "rw": a["L0_ffn_router_w"].T,
        "ln_scale": a["L0_xattn_ln_scale"],
        "g_xattn": a["g_xattn"].reshape(1),
        "g_ffn": a["g_ffn"].reshape(1),
        "eg": a["L0_ffn_gate_w"],
        "eu": a["L0_ffn_up_w"],
        "ed": a["L0_ffn_down_w"],
        "sg": a["L0_ffn_shared_gate_w"],
        "su": a["L0_ffn_shared_up_w"],
        "sd": a["L0_ffn_shared_down_w"],
    }
    nc = _bacc.Bacc("TRN2", target_bir_lowering=False, num_devices=1)
    f32, i32 = _mybir.dt.float32, _mybir.dt.int32
    arrays, t = {}, {}
    for name, value in given.items():
        value = _np.ascontiguousarray(value)
        arrays[f"in_{name}"] = value
        t[name] = nc.dram_tensor(f"in_{name}", value.shape, _mybir.dt.from_np(value.dtype), kind="ExternalInput").ap()
    for name, shape, dt in (("x1", (T, D), f32), ("xn", (T, D), f32), ("z", (T, D), f32), ("g_row", (NH, P), f32),
                            ("lists", (NE * CAP + P, 1), i32), ("y", (MAX_TILES * P, D), f32)):
        t[name] = nc.dram_tensor(f"mid_{name}", shape, dt, kind="Internal").ap()
    out = nc.dram_tensor("out_0", (T, D), f32, kind="ExternalOutput").ap()
    t["out"] = out
    build(nc, t)
    r = _run(nc, [arrays], core_ids=[0])
    return r.results[0]["out_0"].reshape(B, S, D)
```
